# Optimizing a Trainium2 kernel written in Bass

```python
import numpy as np
import jax
import jax.numpy as jnp

def _softmax(x, axis=-1):
    return jax.nn.softmax(x, axis=axis)

def _gelu(x):
    return jax.nn.gelu(x, approximate=True)

def _silu(x):
    return jax.nn.silu(x)

def _sigmoid(x):
    return jax.nn.sigmoid(x)

def _layernorm(x, axis=-1, eps=1e-05):
    m = jnp.mean(x, axis=axis, keepdims=True)
    v = jnp.var(x, axis=axis, keepdims=True)
    return (x - m) / jnp.sqrt(v + eps)

def _scatter_add(tgt, idx, src, axis=0):
    return tgt.at[idx].add(src)

def _segment_sum(src, seg, n):
    return jax.ops.segment_sum(src, seg, n)
kernel_name = 'mk_seq_postln_d1_jaxref_r8_bbc902'

def setup_inputs(seed: int=0):
    np.random.seed(seed)
    _w = jnp.asarray

    def _L0_attn_setup():
        import jax, jax.numpy as jnp
        import numpy as np
        B, N, D = (4, 256, 128)
        H, HD = (16, 64)
        MAX_SEQ = 512
        INNER = H * HD

        def _rope_tables(n, head_dim):
            inv_freq = 1.0 / 10000.0 ** (jnp.arange(0, head_dim, 2, dtype=jnp.float32) / head_dim)
            pos = jnp.arange(n, dtype=jnp.float32)
            ang = pos[:, None] * inv_freq[None, :]
            return (jnp.sin(ang), jnp.cos(ang))
        key = jax.random.key(seed)
        ks = jax.random.split(key, 5)
        s = 0.02
        return {'x': jax.random.normal(ks[0], (B, N, D), dtype=jnp.float32), 'ln_gamma': jnp.ones((D,), jnp.float32), 'ln_beta': jnp.zeros((D,), jnp.float32), 'w_qkv': jax.random.normal(ks[1], (D, 3 * INNER), dtype=jnp.float32) * s, 'w_out': jax.random.normal(ks[2], (INNER, D), dtype=jnp.float32) * s, 'b_out': jnp.zeros((D,), jnp.float32)}
    _L0_attn_in = _L0_attn_setup()

    def _L0_ffn_setup():
        import jax, jax.numpy as jnp
        import numpy as np
        TOPK = 4
        key = jax.random.key(seed)
        ks = jax.random.split(key, 9)
        B, T, D = (4, 256, 128)
        E, H = (32, 128)
        HS = H * TOPK
        s = lambda k, shape, fan: jax.random.normal(k, shape, dtype=jnp.float32) / np.sqrt(fan)
        return {'x': jax.random.normal(ks[0], (B, T, D), dtype=jnp.float32), 'router_w': s(ks[1], (E, D), D), 'router_bias': jnp.zeros((E,), dtype=jnp.float32), 'gate_w': s(ks[2], (E, H, D), D), 'up_w': s(ks[3], (E, H, D), D), 'down_w': s(ks[4], (E, D, H), H), 'sgate_w': s(ks[5], (HS, D), D), 'sup_w': s(ks[6], (HS, D), D), 'sdown_w': s(ks[7], (D, HS), HS)}
    _L0_ffn_in = _L0_ffn_setup()
    _d = {'L0_attn_x': _L0_attn_in['x'], 'L0_attn_ln_gamma': _L0_attn_in['ln_gamma'], 'L0_attn_ln_beta': _L0_attn_in['ln_beta'], 'L0_attn_w_qkv': _L0_attn_in['w_qkv'], 'L0_attn_w_out': _L0_attn_in['w_out'], 'L0_attn_b_out': _L0_attn_in['b_out'], 'L0_ffn_router_w': _L0_ffn_in['router_w'], 'L0_ffn_router_bias': _L0_ffn_in['router_bias'], 'L0_ffn_gate_w': _L0_ffn_in['gate_w'], 'L0_ffn_up_w': _L0_ffn_in['up_w'], 'L0_ffn_down_w': _L0_ffn_in['down_w'], 'L0_ffn_sgate_w': _L0_ffn_in['sgate_w'], 'L0_ffn_sup_w': _L0_ffn_in['sup_w'], 'L0_ffn_sdown_w': _L0_ffn_in['sdown_w']}
    _x0 = _d['L0_attn_x']
    _d['L0_attn_x'] = jax.random.normal(jax.random.fold_in(jax.random.key(seed), 1), (4, 512, 128), dtype=_x0.dtype)
    del _x0
    return _d

def reference(L0_attn_x, L0_attn_ln_gamma, L0_attn_ln_beta, L0_attn_w_qkv, L0_attn_w_out, L0_attn_b_out, L0_ffn_router_w, L0_ffn_router_bias, L0_ffn_gate_w, L0_ffn_up_w, L0_ffn_down_w, L0_ffn_sgate_w, L0_ffn_sup_w, L0_ffn_sdown_w):

    def _L0_attn_ref(x, ln_gamma, ln_beta, w_qkv, w_out, b_out):
        import jax, jax.numpy as jnp
        import numpy as np
        B, N, D = (4, 256, 128)
        H, HD = (16, 64)
        MAX_SEQ = 512
        INNER = H * HD

        def _rope_tables(n, head_dim):
            inv_freq = 1.0 / 10000.0 ** (jnp.arange(0, head_dim, 2, dtype=jnp.float32) / head_dim)
            pos = jnp.arange(n, dtype=jnp.float32)
            ang = pos[:, None] * inv_freq[None, :]
            return (jnp.sin(ang), jnp.cos(ang))
        b, n, d = x.shape
        mu = jnp.mean(x, axis=-1, keepdims=True)
        var = jnp.var(x, axis=-1, keepdims=True)
        xn = (x - mu) / jnp.sqrt(var + 1e-05) * ln_gamma + ln_beta
        qkv = xn @ w_qkv
        q, k, v = jnp.split(qkv, 3, axis=-1)

        def to_heads(t):
            return t.reshape(b, n, H, HD).transpose(0, 2, 1, 3)
        q, k, v = (to_heads(q), to_heads(k), to_heads(v))
        sin, cos = _rope_tables(n, HD)
        sin = sin[None, None]
        cos = cos[None, None]
        half = HD // 2

        def rotate(t):
            t1, t2 = (t[..., :half], t[..., half:])
            return jnp.concatenate([t1 * cos - t2 * sin, t2 * cos + t1 * sin], axis=-1)
        qr, kr = (rotate(q), rotate(k))
        scale = HD ** (-0.5)
        scores = jnp.einsum('bhid,bhjd->bhij', qr, kr) * scale
        probs = jax.nn.softmax(scores, axis=-1)
        out = jnp.einsum('bhij,bhjd->bhid', probs, v)
        out = out.transpose(0, 2, 1, 3).reshape(b, n, INNER)
        return out @ w_out + b_out

    def _L0_ffn_ref(x, router_w, router_bias, gate_w, up_w, down_w, sgate_w, sup_w, sdown_w):
        import jax, jax.numpy as jnp
        import numpy as np
        TOPK = 4
        B, T, D = x.shape
        flat = x.reshape(B * T, D)
        logits = flat.astype(jnp.float32) @ router_w.T + router_bias
        scores = jax.nn.softmax(logits, axis=-1)
        topk_scores, topk_idx = jax.lax.top_k(scores, TOPK)
        topk_scores = topk_scores / jnp.clip(topk_scores.sum(axis=-1, keepdims=True), 1e-12, None)
        h = jax.nn.silu(jnp.einsum('nd,ehd->neh', flat, gate_w)) * jnp.einsum('nd,ehd->neh', flat, up_w)
        expert_out = jnp.einsum('neh,edh->ned', h, down_w)
        sel = jnp.take_along_axis(expert_out, topk_idx[:, :, None], axis=1)
        out = (sel * topk_scores.astype(flat.dtype)[:, :, None]).sum(axis=1)
        out = out + jax.nn.silu(flat @ sgate_w.T) * (flat @ sup_w.T) @ sdown_w.T
        return out.reshape(B, T, D)
    x = L0_attn_x
    x = _layernorm(x + _L0_attn_ref(x, L0_attn_ln_gamma, L0_attn_ln_beta, L0_attn_w_qkv, L0_attn_w_out, L0_attn_b_out), axis=-1)
    x = _layernorm(x + _L0_ffn_ref(x, L0_ffn_router_w, L0_ffn_router_bias, L0_ffn_gate_w, L0_ffn_up_w, L0_ffn_down_w, L0_ffn_sgate_w, L0_ffn_sup_w, L0_ffn_sdown_w), axis=-1)
    return x

_drawn_inputs = setup_inputs


def setup_inputs(seed=0):
    import zlib

    import numpy as np

    out = dict(_drawn_inputs(seed))
    spreads = {'L0_attn_ln_gamma': (1.0, 0.2),
     'L0_attn_ln_beta': (0.0, 0.1),
     'L0_attn_b_out': (0.0, 0.1),
     'L0_ffn_router_bias': (0.0, 0.1)}
    factors = {}
    for name, (base, spread) in spreads.items():
        noise = np.random.default_rng([zlib.crc32(name.encode()), seed]).standard_normal(out[name].shape)
        drawn = base * np.exp(spread * noise) if base else spread * noise
        out[name] = jnp.asarray(drawn.astype(out[name].dtype))
    for name, factor in factors.items():
        out[name] = (out[name] * factor).astype(out[name].dtype)
    return out
```

```python
from contextlib import ExitStack

import numpy as np

import concourse.bass as bass
from concourse import mybir

F32 = mybir.dt.float32
F32R = mybir.dt.float32r
ALU = mybir.AluOpType
ACT = mybir.ActivationFunctionType
AX_X = mybir.AxisListType.X

P = 128
BATCH, SEQ, D = 4, 512, 128
HEADS, HEAD_DIM = 16, 64
TILES = SEQ // P
PAIRS = HEADS // 2
HEAD_SLOTS = BATCH * HEADS
EXPERTS, HIDDEN, TOP_K = 32, 128, 4
SHARED = 4
BLOCKS = EXPERTS + SHARED
ITEMS = BLOCKS * BATCH
EPS = 1e-5
HALF = HEAD_DIM // 2


def positive(eng, sem, value):
    if not isinstance(value, int) or value > 0:
        eng.wait_ge(sem, value)


def run_slots(eng, slot, total, early, late):
    turns = total // 8
    for n in range(-early, 8):
        slot(n // 8, n % 8, lambda k, n=n: 0 <= n + k < total)
    with eng.Fori(1, turns - 1) as h:
        for r in range(8):
            slot(h, r, lambda k: True)
    for n in range(total - 8, total + late):
        slot(n // 8, n % 8, lambda k, n=n: 0 <= n + k < total)


def layer_program(nc, x, gamma, beta, wqkv, wout, bout, rope, router_w, router_b, ffn_w, out):
    with ExitStack() as ctx:
        def sb(name, shape, dt=F32):
            return ctx.enter_context(nc.sbuf_tensor(name, shape, dt))

        def sem(name):
            return ctx.enter_context(nc.semaphore(name))

        psum = ctx.enter_context(nc.psum_tensor("psum", [P, 8, 512], F32))

        ident = sb("ident", [P, P])
        gamma_c = sb("gamma_c", [P, 1])
        beta_c = sb("beta_c", [P, 1])
        eps_c = sb("eps_c", [P, 1])
        ones_c = sb("ones_c", [P, 1])
        bout_row = sb("bout_row", [P, D])
        rbias_row = sb("rbias_row", [P, EXPERTS])
        router_sb = sb("router_sb", [D, EXPERTS])
        rope_sb = sb("rope_sb", [P, 2, 2, SEQ])

        x_tok = sb("x_tok", [P, BATCH * TILES, D])
        sum_tok = sb("sum_tok", [P, BATCH * TILES, D])
        stats = sb("stats", [P, BATCH * TILES, 6])
        mean_var = sb("mean_var", [P, BATCH * TILES, 2])
        std = sb("std", [P, BATCH * TILES, 1])

        xT = sb("xT", [P, BATCH, SEQ])
        xT_hi = sb("xT_hi", [P, BATCH, SEQ], F32R)
        xT_lo = sb("xT_lo", [P, BATCH, SEQ], F32R)
        yT = sb("yT", [P, BATCH, SEQ])

        wqkv_raw = sb("wqkv_raw", [P, 3, P])
        wqkv_hi = sb("wqkv_hi", [P, 3, P], F32R)
        wqkv_lo = sb("wqkv_lo", [P, 3, P], F32R)
        wout_raw = sb("wout_raw", [P, 2, D])
        wout_hi = sb("wout_hi", [P, 2, D], F32R)
        wout_lo = sb("wout_lo", [P, 2, D], F32R)
        qk_flat = sb("qk_flat", [P, 2, SEQ])
        qk_swap = sb("qk_swap", [P, 2, SEQ])
        qk_hi = sb("qk_hi", [P, 2, SEQ], F32R)
        qk_lo = sb("qk_lo", [P, 2, SEQ], F32R)
        stacks = sb("stacks", [P, 2, 2, 3, SEQ], F32R)
        v_flat = sb("v_flat", [P, SEQ])
        v_parts = sb("v_parts", [P, 4, 2, TILES, P], F32R)
        neg_max = sb("neg_max", [P, 4, TILES])
        row_sum = sb("row_sum", [P, 4, TILES])
        inv_sum = sb("inv_sum", [P, 4, TILES])
        probs = sb("probs", [P, 4, TILES, SEQ])
        probsT_hi = sb("probsT_hi", [P, TILES, SEQ], F32R)
        probsT_lo = sb("probsT_lo", [P, TILES, SEQ], F32R)
        headT_hi = sb("headT_hi", [P, 2, SEQ], F32R)
        headT_lo = sb("headT_lo", [P, 2, SEQ], F32R)

        logits = sb("logits", [P, 16, EXPERTS])
        row_stat = sb("row_stat", [P, 4, 16])
        SENT = EXPERTS + 4
        scores_r = sb("scores_r", [P, 16, SENT])
        marked = sb("marked", [P, 16, SENT])
        top8 = sb("top8", [P, 16, 8])
        weights_tok = probs[:, 0, :, :].rearrange("p t (a e) -> p (t a) e", e=P)
        weightsT = sb("weightsT", [P, BATCH, SEQ], F32R)

        ffn_raw = sb("ffn_raw", [P, 2, 3, P])
        ffn_hi = sb("ffn_hi", [P, 2, 3, P], F32R)
        ffn_lo = sb("ffn_lo", [P, 2, 3, P], F32R)
        pick = sb("pick", [P, BLOCKS])
        pick_wide = sb("pick_wide", [P, 2, P], F32R)
        silu = probs[:, 1, 0:2, :]
        hidden = probs[:, 1, 2:4, :]
        hidden_w = probs[:, 2, 0:2, :]
        hidden_hi = probsT_hi[:, 0:2, :]
        hidden_lo = probsT_lo[:, 0:2, :]

        x_in = [sem(f"x_in{b}") for b in range(BATCH)]
        consts_in = sem("consts_in")
        ident_step = sem("ident_step")
        eps_set = sem("eps_set")
        back_turned = sem("back_turned")
        summed = sem("summed")
        stats_done = sem("stats_done")
        var_done = sem("var_done")
        std_done = sem("std_done")
        rstd_done = sem("rstd_done")
        normed = sem("normed")
        norm_turned = sem("norm_turned")
        xT_done = sem("xT_done")
        xT_hi_done = sem("xT_hi_done")
        xT_lo_done = sem("xT_lo_done")
        resid_done = sem("resid_done")
        out_done = sem("out_done")
        wqkv_in = sem("wqkv_in")
        wout_in = sem("wout_in")
        wq_staged = [sem(f"wqkv_staged{m}") for m in range(3)]
        wo_staged = sem("wo_staged")
        wq_step = sem("wq_step")
        q_projected, k_projected, v_projected = sem("q_projected"), sem("k_projected"), sem("v_projected")
        q_flat_done, k_flat_done, v_flat_done = sem("q_flat_done"), sem("k_flat_done"), sem("v_flat_done")
        swapped = [sem("q_swapped"), sem("k_swapped")]
        rope_step = sem("rope_step")
        rotated = [sem("q_rotated"), sem("k_rotated")]
        stacked = [sem("q_stacked"), sem("k_stacked")]
        v_turned = sem("v_turned")
        v_hi_done, v_lo_done = sem("v_hi_done"), sem("v_lo_done")
        scored = sem("scored")
        maxed = sem("maxed")
        exped = sem("exped")
        inverted = sem("inverted")
        normalised = sem("normalised")
        probs_turned = sem("probs_turned")
        probsT_hi_done, probsT_lo_done = sem("probsT_hi_done"), sem("probsT_lo_done")
        mixed = sem("mixed")
        headT_hi_done, headT_lo_done = sem("headT_hi_done"), sem("headT_lo_done")
        head_projected = sem("head_projected")
        y_added = sem("y_added")
        r_logits = sem("r_logits")
        r_step = sem("r_step")
        r_exp = sem("r_exp")
        r_sent = sem("r_sent")
        weights_done = sem("weights_done")
        weights_turned = sem("weights_turned")
        weightsT_copied = sem("weightsT_copied")
        weightsT_done = sem("weightsT_done")
        pick_step = sem("pick_step")
        ffn_in = [sem("ffn_in0"), sem("ffn_in1")]
        ffn_step = sem("ffn_step")
        ffn_staged = sem("ffn_staged")
        gated, upped, spread = sem("gated"), sem("upped"), sem("spread")
        silu_done = sem("silu_done")
        hidden_done = sem("hidden_done")
        hidden_w_done = sem("hidden_w_done")
        hidden_hi_done, hidden_lo_done = sem("hidden_hi_done"), sem("hidden_lo_done")
        downed = sem("downed")
        ffn_y_out = sem("ffn_y_out")

        x_dram = x.rearrange("b (t p) d -> p b t d", p=P)
        out_dram = out.rearrange("b (t p) d -> p b t d", p=P)
        CONSTS = 16 * 7

        block = ctx.enter_context(nc.Block())

        def tiles_of(b):
            return slice(TILES * b, TILES * (b + 1))

        @block.sync
        def _(sp):
            for b in range(BATCH):
                sp.dma_start(x_tok[:, tiles_of(b), :], x_dram[:, b, :, :]).then_inc(x_in[b], 16)
                if b == 0:
                    sp.dma_start(wqkv_raw[:], wqkv[:, 0, :, :]).then_inc(wqkv_in, 16)
                    sp.dma_start(wout_raw[:], wout[:, 0, :, :]).then_inc(wout_in, 16)
            sp.dma_start(gamma_c[:], gamma).then_inc(consts_in, 16)
            sp.dma_start(beta_c[:], beta).then_inc(consts_in, 16)
            sp.dma_start(rope_sb[:], rope).then_inc(consts_in, 16)
            sp.dma_start(bout_row[:], bout).then_inc(consts_in, 16)
            sp.dma_start(rbias_row[:], router_b).then_inc(consts_in, 16)
            sp.dma_start(router_sb[:], router_w).then_inc(consts_in, 16)
            sp.dma_start(ffn_raw[:], ffn_w[:, 0:2, :, :]).then_inc(consts_in, 16)

            def value(v):
                if not isinstance(v, int):
                    sp.compute_val(v)
                return v

            def wait_all(*waits):
                for s, v in [(s, value(v)) for s, v in waits]:
                    positive(sp, s, v)

            def swap(m, done, w):
                wait_all((done, w + 1), (rotated[m], w))
                for piece in range(4):
                    src = HALF * piece
                    dst = HALF * (piece ^ 1)
                    sp.dma_start(qk_swap[dst:dst + HALF, m, :], qk_flat[src:src + HALF, m, :])\
                        .then_inc(swapped[m], 16)

            def stack(m, w, buf):
                wait_all((rotated[m], w + 1), (scored, 8 * w - 8))
                for s in range(2):
                    rows = slice(HEAD_DIM * s, HEAD_DIM * (s + 1))
                    top, low = slice(0, HEAD_DIM), slice(HEAD_DIM, P)
                    moves = [(stacks[top, buf, s, m, :], qk_hi), (stacks[low, buf, s, m, :], qk_lo)]
                    if m == 1:
                        moves += [(stacks[top, buf, s, 2, :], qk_lo), (stacks[low, buf, s, 2, :], qk_hi)]
                    for dst, src in moves:
                        sp.dma_start(dst.bitcast(F32), src[rows, m, :].bitcast(F32)).then_inc(stacked[m], 16)

            def slot(h, r, live):
                if r % 2 == 1 and live(3):
                    swap(0, q_flat_done, 4 * h + (r + 3) // 2)
                if r % 2 == 0 and live(2):
                    w, buf = 4 * h + (r + 2) // 2, (r + 2) // 2 % 2
                    swap(1, k_flat_done, w)
                    stack(0, w, buf)
                    stack(1, w, buf)
                if r == 0 and live(8):
                    nxt = value(h + 1)
                    for m in range(3):
                        sp.wait_ge(wq_staged[m], nxt)
                    sp.dma_start(wqkv_raw[:], wqkv[:, bass.ds(nxt, 1), :, :].rearrange("p a m n -> p (a m) n"))\
                        .then_inc(wqkv_in, 16)
                if r == 5 and live(0) and live(3):
                    nxt = value(h + 1)
                    sp.wait_ge(wo_staged, nxt)
                    sp.dma_start(wout_raw[:], wout[:, bass.ds(nxt, 1), :, :].rearrange("p a m n -> p (a m) n"))\
                        .then_inc(wout_in, 16)

            run_slots(sp, slot, HEAD_SLOTS, 3, 3)

            for par in range(2):
                sp.wait_ge(ffn_staged, par + 1)
                sp.dma_start(ffn_raw[:, par, :, :], ffn_w[:, 2 + par, :, :]).then_inc(ffn_in[par], 16)
            with sp.Fori(1, BLOCKS // 2 - 1) as h:
                for par in range(2):
                    block_no, count = value(2 * h + (2 + par)), value(2 * h + (par + 1))
                    sp.wait_ge(ffn_staged, count)
                    sp.dma_start(ffn_raw[:, par, :, :],
                                 ffn_w[:, bass.ds(block_no, 1), :, :].rearrange("p a m n -> p (a m) n"))\
                        .then_inc(ffn_in[par], 16)

            for b in range(BATCH):
                sp.wait_ge(normed, 2 * BATCH + b + 1)
                sp.dma_start(out_dram[:, b, :, :], sum_tok[:, tiles_of(b), :]).then_inc(out_done, 16)
            sp.wait_ge(out_done, 16 * BATCH)

        @block.tensor
        def _(pe):
            def three(dst, w_hi, w_lo, m_hi, m_lo, start=True, stop=True):
                nc.tensor.matmul(dst, w_lo, m_hi, start=start, stop=False)
                nc.tensor.matmul(dst, w_hi, m_lo, start=False, stop=False)
                return nc.tensor.matmul(dst, w_hi, m_hi, start=False, stop=stop)

            def turn_normed(norm):
                for b in range(BATCH):
                    pe.wait_ge(normed, BATCH * norm + b + 1)
                    for i in range(TILES):
                        mm = nc.tensor.transpose(psum[:, b, i * P:(i + 1) * P], sum_tok[:, TILES * b + i, :], ident[:])
                    mm.then_inc(norm_turned, 1)

            def turn_back(b):
                for i in range(TILES):
                    mm = nc.tensor.transpose(psum[:, 4 + b, i * P:(i + 1) * P], yT[:, b, i * P:(i + 1) * P], ident[:])
                mm.then_inc(back_turned, 1)

            pe.wait_ge(ident_step, 2)
            turn_normed(0)
            pe.wait_ge(xT_lo_done, BATCH)

            def slot(h, r, live):
                t = 8 * h + r
                for q in range(TILES):
                    c = 4 * t + q
                    if live(-2):
                        if q == 0:
                            pe.wait_ge(normalised, t - 1)
                        positive(pe, probsT_lo_done, c - 8 - 1)
                        for i in range(TILES):
                            mm = nc.tensor.transpose(psum[:, 2 + q % 2, i * P:(i + 1) * P],
                                                     probs[:, (r - 2) % 4, i, q * P:(q + 1) * P], ident[:])
                        mm.then_inc(probs_turned, 1)
                    if live(0):
                        if q == 0 and r % 2 == 0:
                            w = 4 * h + r // 2
                            pe.wait_ge(stacked[0], 64 * w + 64)
                            pe.wait_ge(stacked[1], 128 * w + 128)
                        positive(pe, exped, c - 1)
                        st = stacks[:, r // 2 % 2, r % 2]
                        lhs = st[:, 0, q * P:(q + 1) * P]
                        nc.tensor.matmul(psum[:, q % 2, :], lhs, st[:, 2, :], start=True, stop=False)
                        nc.tensor.matmul(psum[:, q % 2, :], lhs, st[:, 1, :], start=False, stop=True)\
                            .then_inc(scored, 1)
                    back = 2 if q >= 2 else 3
                    if live(-back):
                        j, rr = (q + 2) % 4, (r - back) % 8
                        pe.wait_ge(probsT_lo_done, c - 10 + 1)
                        if j == 0:
                            positive(pe, headT_lo_done, t - back - 1)
                            pair = 4 * h + (r - back) // 2
                            pe.wait_ge(v_lo_done, pair + 1)
                        lhs = v_parts[:, rr // 2, rr % 2, j, :]
                        dst = psum[:, 4 + rr % 2, :]
                        nc.tensor.matmul(dst, lhs, probsT_lo[:, j, :], start=(j == 0), stop=False)
                        nc.tensor.matmul(dst, lhs, probsT_hi[:, j, :], start=False, stop=(j == 3))\
                            .then_inc(mixed, 1)
                    if r % 2 == 1 and live(3):
                        b = (r + 3) // 2 % 4
                        w = 4 * h + (r + 3) // 2
                        if q == 1:
                            positive(pe, v_lo_done, w)
                            pe.wait_ge(wq_staged[0], h + 1 + (r + 3) // 8)
                            three(psum[:, 6, :], wqkv_hi[:, 0, :], wqkv_lo[:, 0, :], xT_hi[:, b, :],
                                  xT_lo[:, b, :]).then_inc(q_projected, 1)
                        if q == 3:
                            pe.wait_ge(q_flat_done, w + 1)
                            pe.wait_ge(wq_staged[1], h + 1 + (r + 3) // 8)
                            three(psum[:, 6, :], wqkv_hi[:, 1, :], wqkv_lo[:, 1, :], xT_hi[:, b, :],
                                  xT_lo[:, b, :]).then_inc(k_projected, 1)
                    if r % 2 == 0 and live(2):
                        b = (r + 2) // 2 % 4
                        w = 4 * h + (r + 2) // 2
                        if q == 1:
                            pe.wait_ge(k_flat_done, w + 1)
                            pe.wait_ge(wq_staged[2], h + 1 + (r + 2) // 8)
                            three(psum[:, 6, :], wqkv_hi[:, 2, :], wqkv_lo[:, 2, :], xT_hi[:, b, :],
                                  xT_lo[:, b, :]).then_inc(v_projected, 1)
                        if q == 3:
                            pe.wait_ge(v_flat_done, w + 1)
                            for i in range(TILES):
                                mm = nc.tensor.transpose(psum[:, 6, i * P:(i + 1) * P],
                                                         v_flat[:, i * P:(i + 1) * P], ident[:])
                            mm.then_inc(v_turned, 1)
                    if q == 3 and live(-3):
                        s = (r - 3) % 2
                        pe.wait_ge(headT_lo_done, t - 3 + 1)
                        pe.wait_ge(wo_staged, h + 1 + (r - 3) // 8)
                        if s == 0:
                            pe.wait_ge(y_added, BATCH + 4 * h + (r - 3) // 2)
                        three(psum[:, 7, :], wout_hi[:, s, :], wout_lo[:, s, :], headT_hi[:, s, :],
                              headT_lo[:, s, :], start=(s == 0), stop=(s == 1)).then_inc(head_projected, 1)

            run_slots(pe, slot, HEAD_SLOTS, 3, 3)

            pe.wait_ge(y_added, BATCH + HEAD_SLOTS // 2)
            for b in range(BATCH):
                turn_back(b)
            turn_normed(1)

            pe.wait_ge(summed, BATCH)
            pe.wait_ge(xT_done, 2 * BATCH)
            for n in range(BATCH * TILES):
                mm = nc.tensor.matmul(psum[:, 7, n * EXPERTS:(n + 1) * EXPERTS],
                                      xT[:, n // TILES, (n % TILES) * P:(n % TILES + 1) * P], router_sb[:],
                                      start=True, stop=True)
            mm.then_inc(r_logits, 1)
            pe.wait_ge(weights_done, 1)
            pe.wait_ge(r_sent, 2)
            pe.wait_ge(xT_lo_done, 2 * BATCH)
            for b in range(BATCH):
                for i in range(TILES):
                    mm = nc.tensor.transpose(psum[:, b, i * P:(i + 1) * P], weights_tok[:, TILES * b + i, :],
                                             ident[:])
                mm.then_inc(weights_turned, 1)

            def ffn_slot(h, r, live):
                k, par, b = 8 * h + r, r // 4, r % 4
                if live(0):
                    if b == 0:
                        pe.wait_ge(ffn_staged, 2 * h + par + 1)
                    positive(pe, silu_done, k)
                    three(psum[:, 4, :], ffn_hi[:, par, 0, :], ffn_lo[:, par, 0, :], xT_hi[:, b, :],
                          xT_lo[:, b, :]).then_inc(gated, 1)
                    positive(pe, hidden_done, k)
                    three(psum[:, 5, :], ffn_hi[:, par, 1, :], ffn_lo[:, par, 1, :], xT_hi[:, b, :],
                          xT_lo[:, b, :]).then_inc(upped, 1)
                    if isinstance(k, int) and k < BATCH:
                        pe.wait_ge(weightsT_done, BATCH)
                    positive(pe, hidden_w_done, k)
                    nc.tensor.matmul(psum[:, 6, :], pick_wide[:, par, :], weightsT[:, b, :],
                                     start=True, stop=True).then_inc(spread, 1)
                if live(-2):
                    r2 = (r - 2) % 8
                    par2, b2 = r2 // 4, r2 % 4
                    first = isinstance(k, int) and k - 2 < BATCH
                    last = isinstance(k, int) and k - 2 >= ITEMS - BATCH
                    pe.wait_ge(hidden_lo_done, k - 2 + 1)
                    three(psum[:, b2, :], ffn_hi[:, par2, 2, :], ffn_lo[:, par2, 2, :], hidden_hi[:, r2 % 2, :],
                          hidden_lo[:, r2 % 2, :], start=first, stop=last).then_inc(downed, 1)

            run_slots(pe, ffn_slot, ITEMS, 0, 2)

            pe.wait_ge(hidden_w_done, ITEMS)
            for b in range(BATCH):
                pe.wait_ge(ffn_y_out, b + 1)
                turn_back(b)

        @block.scalar
        def _(act):
            def norm_std(norm):
                for b in range(BATCH):
                    act.wait_ge(var_done, BATCH * norm + b + 1)
                    if norm == 0 and b == 0:
                        act.wait_ge(eps_set, 1)
                    nc.scalar.activation(std[:, tiles_of(b), :], mean_var[:, tiles_of(b), 1:2], ACT.Sqrt,
                                         bias=eps_c[:, 0:1]).then_inc(std_done, 1)

            def high_parts(norm):
                for b in range(BATCH):
                    act.wait_ge(xT_done, BATCH * norm + b + 1)
                    nc.scalar.activation(xT_hi[:, b, :], xT[:, b, :], ACT.Copy).then_inc(xT_hi_done, 1)

            norm_std(0)
            high_parts(0)

            def slot(h, r, live):
                t = 8 * h + r
                for q in range(TILES):
                    c = 4 * t + q
                    if live(-2):
                        act.wait_ge(probs_turned, c - 8 + 1)
                        positive(act, mixed, c - 8 - 3)
                        nc.scalar.activation(probsT_hi[:, q, :], psum[:, 2 + q % 2, :], ACT.Copy)\
                            .then_inc(probsT_hi_done, 1)
                    if live(0):
                        act.wait_ge(maxed, c + 1)
                        if q == 0:
                            positive(act, probs_turned, 4 * t - 12)
                        nc.scalar.activation(probs[:, r % 4, q, :], psum[:, q % 2, :], ACT.Exp,
                                             bias=neg_max[:, r % 4, q:q + 1],
                                             accum_out=row_sum[:, r % 4, q:q + 1]).then_inc(exped, 1)
                    if q == 1 and live(-3):
                        act.wait_ge(mixed, 4 * t - 8)
                        positive(act, head_projected, t - 3 - 1)
                        nc.scalar.activation(headT_hi[:, (r - 3) % 2, :], psum[:, 4 + (r - 3) % 2, :], ACT.Copy)\
                            .then_inc(headT_hi_done, 1)
                    if r % 2 == 1 and q == 2 and live(3):
                        w = 4 * h + (r + 3) // 2
                        act.wait_ge(q_projected, w + 1)
                        positive(act, rotated[0], w)
                        nc.scalar.activation(qk_flat[:, 0, :], psum[:, 6, :], ACT.Copy).then_inc(q_flat_done, 1)
                    if r % 2 == 0 and live(2):
                        w = 4 * h + (r + 2) // 2
                        if q == 0:
                            act.wait_ge(k_projected, w + 1)
                            positive(act, rotated[1], w)
                            nc.scalar.activation(qk_flat[:, 1, :], psum[:, 6, :], ACT.Copy)\
                                .then_inc(k_flat_done, 1)
                        if q == 2:
                            act.wait_ge(v_projected, w + 1)
                            positive(act, v_turned, w)
                            nc.scalar.activation(v_flat[:], psum[:, 6, :], ACT.Copy).then_inc(v_flat_done, 1)
                    if r % 2 == 1 and q == 0 and live(1):
                        w, buf = 4 * h + (r + 1) // 2, (r + 1) // 2 % 4
                        act.wait_ge(v_turned, w + 1)
                        positive(act, mixed, 8 * w - 24)
                        nc.scalar.activation(
                            v_parts[:, buf, :, :, 0:HEAD_DIM].rearrange("p s i d -> p i s d"),
                            psum[:, 6, :].rearrange("p (i s d) -> p i s d", i=TILES, s=2),
                            ACT.Copy).then_inc(v_hi_done, 1)

            run_slots(act, slot, HEAD_SLOTS, 3, 3)

            norm_std(1)
            for b in range(BATCH):
                act.wait_ge(norm_turned, BATCH + b + 1)
                nc.scalar.activation(xT[:, b, :], psum[:, b, :], ACT.Copy).then_inc(xT_done, 1)
            high_parts(1)
            act.wait_ge(r_step, 3)
            nc.scalar.activation(scores_r[:, :, 0:EXPERTS], logits[:], ACT.Exp).then_inc(r_exp, 1)
            for b in range(BATCH):
                act.wait_ge(weights_turned, b + 1)
                nc.scalar.activation(weightsT[:, b, :], psum[:, b, :], ACT.Copy).then_inc(weightsT_copied, 1)

            def ffn_slot(h, r, live):
                if live(0):
                    k = 8 * h + r
                    act.wait_ge(gated, k + 1)
                    positive(act, hidden_done, k - 1)
                    nc.scalar.activation(silu[:, r % 2, :], psum[:, 4, :], ACT.Silu).then_inc(silu_done, 1)
                    act.wait_ge(hidden_w_done, k + 1)
                    positive(act, downed, k - 1)
                    nc.scalar.activation(hidden_hi[:, r % 2, :], hidden_w[:, r % 2, :], ACT.Copy)\
                        .then_inc(hidden_hi_done, 1)

            run_slots(act, ffn_slot, ITEMS, 0, 0)

            for b in range(BATCH):
                act.wait_ge(downed, ITEMS - BATCH + b + 1)
                nc.scalar.activation(yT[:, b, :], psum[:, b, :], ACT.Copy).then_inc(ffn_y_out, 1)
            norm_std(2)

        @block.vector
        def _(dve):
            def norm_stats(norm, b):
                for n in range(TILES * b, TILES * (b + 1)):
                    ins = nc.vector.bn_stats(stats[:, n, :], (x_tok if norm == 0 else sum_tok)[:, n, :])
                ins.then_inc(stats_done, 1)
                dve.wait_ge(stats_done, BATCH * norm + b + 1)
                for n in range(TILES * b, TILES * (b + 1)):
                    ins = nc.vector.bn_aggr(mean_var[:, n, :], stats[:, n, :])
                ins.then_inc(var_done, 1)

            def norm_apply(norm, b):
                dve.wait_ge(std_done, BATCH * norm + b + 1)
                nc.vector.reciprocal(std[:, tiles_of(b), :], std[:, tiles_of(b), :]).then_inc(rstd_done, 1)
                dve.wait_ge(rstd_done, BATCH * norm + b + 1)
                for n in range(TILES * b, TILES * (b + 1)):
                    ins = nc.vector.tensor_scalar(sum_tok[:, n, :], (x_tok if norm == 0 else sum_tok)[:, n, :],
                                                  mean_var[:, n, 0:1], std[:, n, :], ALU.subtract, ALU.mult)
                ins.then_inc(normed, 1)

            def add_back(norm, b):
                dve.wait_ge(back_turned, BATCH * (norm - 1) + b + 1)
                nc.vector.tensor_tensor(sum_tok[:, tiles_of(b), :],
                                        psum[:, 4 + b, :].rearrange("p (i d) -> p i d", i=TILES),
                                        x_tok[:, tiles_of(b), :], ALU.add).then_inc(summed, 1)
                dve.wait_ge(summed, BATCH * (norm - 1) + b + 1)

            nc.vector.memset(eps_c[:], EPS).then_inc(eps_set, 1)
            for b in range(BATCH):
                dve.wait_ge(x_in[b], 16)
                norm_stats(0, b)
            for b in range(BATCH):
                norm_apply(0, b)
            dve.wait_ge(consts_in, CONSTS)
            for b in range(BATCH):
                dve.wait_ge(norm_turned, b + 1)
                nc.vector.tensor_scalar(xT[:, b, :], psum[:, b, :], gamma_c[:, 0:1], beta_c[:, 0:1],
                                        ALU.mult, ALU.add).then_inc(xT_done, 1)
            for b in range(BATCH):
                dve.wait_ge(xT_hi_done, b + 1)
                nc.vector.tensor_tensor(xT_lo[:, b, :], xT[:, b, :], xT_hi[:, b, :].bitcast(F32),
                                        ALU.subtract).then_inc(xT_lo_done, 1)
            for b in range(BATCH):
                nc.vector.memset(yT[:, b, :], 0.0).then_inc(y_added, 1)

            def slot(h, r, live):
                t = 8 * h + r
                for q in range(TILES):
                    c = 4 * t + q
                    if live(0):
                        dve.wait_ge(scored, c + 1)
                        if q == 0:
                            positive(dve, exped, 4 * t - 12)
                        nc.vector.tensor_reduce(neg_max[:, r % 4, q:q + 1], psum[:, q % 2, :], AX_X, ALU.max,
                                                negate=True).then_inc(maxed, 1)
                    if live(-2):
                        dve.wait_ge(probsT_hi_done, c - 8 + 1)
                        nc.vector.tensor_tensor(probsT_lo[:, q, :], psum[:, 2 + q % 2, :],
                                                probsT_hi[:, q, :].bitcast(F32), ALU.subtract)\
                            .then_inc(probsT_lo_done, 1)
                    if q == 0 and live(-1):
                        dve.wait_ge(exped, 4 * t)
                        positive(dve, normalised, t - 4)
                        nc.vector.reciprocal(inv_sum[:, (r - 1) % 4, :], row_sum[:, (r - 1) % 4, :])\
                            .then_inc(inverted, 1)
                    if q == 0 and r % 2 == 1 and live(1):
                        w, buf = 4 * h + (r + 1) // 2, (r + 1) // 2 % 4
                        dve.wait_ge(v_hi_done, w + 1)
                        for s in range(2):
                            ins = nc.vector.tensor_tensor(
                                v_parts[:, buf, s, :, HEAD_DIM:P],
                                psum[:, 6, :].rearrange("p (i s d) -> p i s d", i=TILES, s=2)[:, :, s, :],
                                v_parts[:, buf, s, :, 0:HEAD_DIM].bitcast(F32), ALU.subtract)
                        ins.then_inc(v_lo_done, 1)
                    if q == 2 and live(-3):
                        dve.wait_ge(headT_hi_done, t - 3 + 1)
                        nc.vector.tensor_tensor(headT_lo[:, (r - 3) % 2, :], psum[:, 4 + (r - 3) % 2, :],
                                                headT_hi[:, (r - 3) % 2, :].bitcast(F32), ALU.subtract)\
                            .then_inc(headT_lo_done, 1)
                    if q == 3 and r % 2 == 0 and live(-3):
                        w, b = 4 * h + (r - 3) // 2, (r - 3) // 2 % 4
                        dve.wait_ge(head_projected, 2 * w + 2)
                        dve.wait_ge(y_added, w + 1)
                        nc.vector.tensor_tensor(yT[:, b, :], psum[:, 7, :], yT[:, b, :], ALU.add)\
                            .then_inc(y_added, 1)

            run_slots(dve, slot, HEAD_SLOTS, 3, 3)

            dve.wait_ge(resid_done, 1)
            for b in range(BATCH):
                add_back(1, b)
                norm_stats(1, b)
            for b in range(BATCH):
                norm_apply(1, b)
            for b in range(BATCH):
                dve.wait_ge(xT_hi_done, BATCH + b + 1)
                nc.vector.tensor_tensor(xT_lo[:, b, :], xT[:, b, :], xT_hi[:, b, :].bitcast(F32),
                                        ALU.subtract).then_inc(xT_lo_done, 1)

            step = [0]

            def chain(ins):
                step[0] += 1
                ins.then_inc(r_step, 1)
                dve.wait_ge(r_step, step[0])

            def wide(v):
                return v.rearrange("p (n a) -> p n a", a=1).broadcast_to([P, 16, EXPERTS])

            best, total = row_stat[:, 0, :], row_stat[:, 1, :]
            dve.wait_ge(r_logits, 1)
            chain(nc.vector.tensor_tensor(logits[:], psum[:, 7, :].rearrange("p (n e) -> p n e", e=EXPERTS),
                                          rbias_row[:].rearrange("p (a e) -> p a e", a=1)
                                          .broadcast_to([P, 16, EXPERTS]), ALU.add))
            chain(nc.vector.tensor_reduce(best, logits[:], AX_X, ALU.max))
            chain(nc.vector.tensor_tensor(logits[:], logits[:], wide(best), ALU.subtract))
            dve.wait_ge(r_exp, 1)
            dve.wait_ge(r_sent, 1)
            soft = scores_r[:, :, 0:EXPERTS]
            chain(nc.vector.tensor_reduce(total, soft, AX_X, ALU.add))
            chain(nc.vector.reciprocal(total, total))
            chain(nc.vector.tensor_tensor(soft, soft, wide(total), ALU.mult))
            for n in range(16):
                ins = nc.vector.max(top8[:, n, :], scores_r[:, n, 0:EXPERTS])
            chain(ins)
            chain(nc.vector.memset(top8[:, :, TOP_K:8], -1.0))
            for n in range(16):
                ins = nc.vector.match_replace(marked[:, n, :], top8[:, n, :], scores_r[:, n, :], -2.0)
            chain(ins)
            chosen = weights_tok[:, :, 0:EXPERTS]
            chain(nc.vector.scalar_tensor_tensor(chosen, marked[:, :, 0:EXPERTS], -2.0, soft,
                                                 ALU.is_equal, ALU.mult))
            chain(nc.vector.tensor_reduce(total, chosen, AX_X, ALU.add))
            chain(nc.vector.tensor_scalar(total, total, 1e-12, None, ALU.max))
            chain(nc.vector.reciprocal(total, total))
            chain(nc.vector.tensor_tensor(chosen, chosen, wide(total), ALU.mult))
            nc.vector.tensor_copy(weights_tok[:, :, EXPERTS:2 * EXPERTS], chosen).then_inc(weights_done, 1)
            lo_rows = slice(EXPERTS, 2 * EXPERTS)
            for b in range(BATCH):
                dve.wait_ge(weightsT_copied, b + 1)
                nc.vector.tensor_tensor(weightsT[lo_rows, b, :], psum[lo_rows, b, :],
                                        weightsT[lo_rows, b, :].bitcast(F32), ALU.subtract)\
                    .then_inc(weightsT_done, 1)

            def ffn_slot(h, r, live):
                k = 8 * h + r
                if live(0):
                    dve.wait_ge(silu_done, k + 1)
                    dve.wait_ge(upped, k + 1)
                    nc.vector.tensor_tensor(hidden[:, r % 2, :], psum[:, 5, :], silu[:, r % 2, :], ALU.mult)\
                        .then_inc(hidden_done, 1)
                    dve.wait_ge(spread, k + 1)
                    dve.wait_ge(hidden_done, k + 1)
                    positive(dve, hidden_lo_done, k - 1)
                    nc.vector.tensor_tensor(hidden_w[:, r % 2, :], psum[:, 6, :], hidden[:, r % 2, :], ALU.mult)\
                        .then_inc(hidden_w_done, 1)

            run_slots(dve, ffn_slot, ITEMS, 0, 0)

            for b in range(BATCH):
                add_back(2, b)
                norm_stats(2, b)
            for b in range(BATCH):
                norm_apply(2, b)

        @block.gpsimd
        def _(pool):
            nc.gpsimd.memset(ident[:], 0.0).then_inc(ident_step, 1)
            pool.wait_ge(ident_step, 1)
            nc.gpsimd.affine_select(out=ident[:], in_=ident[:], compare_op=ALU.not_equal, fill=1.0, base=0,
                                    pattern=[[-1, P]], channel_multiplier=1).then_inc(ident_step, 1)
            picks = [0]

            def pick_chain(ins):
                picks[0] += 1
                ins.then_inc(pick_step, 1)
                pool.wait_ge(pick_step, picks[0])

            pick_chain(nc.gpsimd.memset(pick[:], 0.0))
            for first in (0, EXPERTS):
                pick_chain(nc.gpsimd.affine_select(out=pick[:, 0:EXPERTS], in_=pick[:, 0:EXPERTS],
                                                   compare_op=ALU.not_equal, fill=1.0, base=-first,
                                                   pattern=[[-1, EXPERTS]], channel_multiplier=1))
            pick_chain(nc.gpsimd.affine_select(out=pick[:, EXPERTS:BLOCKS], in_=pick[:, EXPERTS:BLOCKS],
                                               compare_op=ALU.not_equal, fill=1.0, base=-2 * EXPERTS,
                                               pattern=[[0, SHARED]], channel_multiplier=1))
            nc.gpsimd.memset(scores_r[:, :, EXPERTS:SENT], -1.0).then_inc(r_sent, 1)
            pick_chain(nc.gpsimd.memset(ones_c[:], 1.0))

            rope_n, wq_n, ffn_n = [0], [0], [0]

            def split(hi, lo, raw, step, base, beside=None):
                one = ones_c[:, 0:1]
                if len(raw.shape) == 3:
                    one = one.rearrange("p (a b) -> p a b", a=1)
                nc.gpsimd.tensor_tensor(hi, raw, one.broadcast_to(list(raw.shape)), ALU.mult).then_inc(step, 1)
                if beside:
                    beside()
                pool.wait_ge(step, base + 1)
                return nc.gpsimd.tensor_tensor(lo, raw, hi.bitcast(F32), ALU.subtract)

            def stage_qkv(m, n):
                pool.wait_ge(wqkv_in, 16 * n + 16)
                used = (q_projected, k_projected, v_projected)[m]
                positive(pool, used, 4 * n)
                split(wqkv_hi[:, m, :], wqkv_lo[:, m, :], wqkv_raw[:, m, :], wq_step, 4 * n + m)\
                    .then_inc(wq_staged[m], 1)

            def stage_out(n):
                pool.wait_ge(wout_in, 16 * n + 16)
                positive(pool, head_projected, 8 * n)
                split(wout_hi[:], wout_lo[:], wout_raw[:], wq_step, 4 * n + 3).then_inc(wo_staged, 1)

            def rotate(m, w):
                done = (q_flat_done, k_flat_done)[m]
                pool.wait_ge(done, w + 1)
                pool.wait_ge(swapped[m], 64 * w + 64)
                base = 6 * w + 3 * m
                nc.gpsimd.tensor_tensor(qk_flat[:, m, :], qk_flat[:, m, :], rope_sb[:, m, 0, :], ALU.mult)
                nc.gpsimd.tensor_tensor(qk_swap[:, m, :], qk_swap[:, m, :], rope_sb[:, m, 1, :], ALU.mult)\
                    .then_inc(rope_step, 2)
                pool.wait_ge(rope_step, base + 2)
                positive(pool, stacked[m], (64 + 64 * m) * w)
                nc.gpsimd.tensor_tensor(qk_hi[:, m, :], qk_flat[:, m, :], qk_swap[:, m, :], ALU.add)
                nc.gpsimd.tensor_tensor(qk_flat[:, m, :], qk_flat[:, m, :], qk_swap[:, m, :], ALU.add)\
                    .then_inc(rope_step, 1)
                pool.wait_ge(rope_step, base + 3)
                nc.gpsimd.tensor_tensor(qk_lo[:, m, :], qk_flat[:, m, :], qk_hi[:, m, :].bitcast(F32),
                                        ALU.subtract).then_inc(rotated[m], 1)

            for m in range(3):
                stage_qkv(m, 0)
            stage_out(0)
            pool.wait_ge(consts_in, CONSTS)

            def slot(h, r, live):
                t = 8 * h + r
                if live(-1):
                    pool.wait_ge(inverted, t)
                    buf = (r - 1) % 4
                    nc.gpsimd.tensor_tensor(probs[:, buf, :, :], probs[:, buf, :, :],
                                            inv_sum[:, buf, :].rearrange("p (i a) -> p i a", a=1)
                                            .broadcast_to([P, TILES, SEQ]), ALU.mult).then_inc(normalised, 1)
                if r % 2 == 0 and live(2):
                    w = 4 * h + (r + 2) // 2
                    rotate(0, w)
                    rotate(1, w)
                if r == 4 and live(8 - 4):
                    stage_qkv(0, h + 1)
                    stage_qkv(1, h + 1)
                    stage_qkv(2, h + 1)
                if r == 3 and live(0) and (not isinstance(h, int) or h >= 1):
                    stage_out(h)

            run_slots(pool, slot, HEAD_SLOTS, 3, 3)

            pool.wait_ge(consts_in, CONSTS)
            nc.gpsimd.tensor_tensor(x_tok[:], x_tok[:], bout_row[:].rearrange("p (a d) -> p a d", a=1)
                                    .broadcast_to([P, BATCH * TILES, D]), ALU.add).then_inc(resid_done, 1)
            pool.wait_ge(probs_turned, 4 * HEAD_SLOTS)
            nc.gpsimd.memset(weights_tok[:, :, 2 * EXPERTS:P], 0.0).then_inc(pick_step, 1)
            pool.wait_ge(pick_step, picks[0] + 1)
            nc.gpsimd.memset(weights_tok[:, :, 2 * EXPERTS:2 * EXPERTS + 1], 1.0).then_inc(r_sent, 1)

            def stage_block(h, par):
                e = 2 * h + par
                if isinstance(h, int) and h == 0:
                    pool.wait_ge(consts_in, CONSTS)
                else:
                    pool.wait_ge(ffn_in[par], 16 * h)
                positive(pool, downed, 4 * e - 4)

                def widen():
                    nc.gpsimd.tensor_copy(pick_wide[:, par, :], pick[:, bass.ds(e, 1)].broadcast_to([P, P]))

                split(ffn_hi[:, par, :, :], ffn_lo[:, par, :, :], ffn_raw[:, par, :, :], ffn_step, e, widen)\
                    .then_inc(ffn_staged, 1)

            stage_block(0, 0)
            stage_block(0, 1)
            pool.wait_ge(normed, 2 * BATCH)
            pool.wait_ge(summed, BATCH)
            nc.gpsimd.tensor_copy(x_tok[:], sum_tok[:]).then_inc(resid_done, 1)

            def ffn_slot(h, r, live):
                k, par = 8 * h + r, r // 4
                if live(0):
                    pool.wait_ge(hidden_hi_done, k + 1)
                    nc.gpsimd.tensor_tensor(hidden_lo[:, r % 2, :], hidden_w[:, r % 2, :],
                                            hidden_hi[:, r % 2, :].bitcast(F32), ALU.subtract)\
                        .then_inc(hidden_lo_done, 1)
                if r % 4 == 2 and live(4) and (not isinstance(h, int) or h > 0 or par == 1):
                    if par == 0:
                        stage_block(h, 1)
                    else:
                        stage_block(h + 1, 0)

            run_slots(pool, ffn_slot, ITEMS, 0, 0)


def rope_tables():
    inv_freq = (np.float32(1.0) / np.float32(10000.0) ** (np.arange(0, HEAD_DIM, 2, dtype=np.float32) / np.float32(HEAD_DIM)))
    ang = np.arange(SEQ, dtype=np.float32)[None, :] * inv_freq.astype(np.float32)[:, None]
    cos, sin = np.cos(ang), np.sin(ang)
    cos = np.concatenate([cos] * 4, 0)
    sin = np.concatenate([-sin, sin] * 2, 0)
    k = np.stack([cos, sin], 1)
    return np.ascontiguousarray(np.stack([k * np.float32(HEAD_DIM ** -0.5), k], 1).astype(np.float32))


def kernel(**inputs):
    import numpy as _np
    import concourse.bacc as _bacc
    from concourse import mybir as _mybir
    from concourse.bass_utils import run_bass_kernel_spmd as _run

    a = {k: _np.asarray(v) for k, v in inputs.items()}
    wqkv = a["L0_attn_w_qkv"].reshape(D, 3, PAIRS, P).transpose(0, 2, 1, 3)
    wo = a["L0_attn_w_out"].reshape(PAIRS, 2, HEAD_DIM, D).transpose(2, 0, 1, 3)
    wo = _np.concatenate([wo, wo], 0)
    gate = _np.concatenate([a["L0_ffn_gate_w"], a["L0_ffn_sgate_w"].reshape(SHARED, HIDDEN, D)], 0).transpose(2, 0, 1)
    up = _np.concatenate([a["L0_ffn_up_w"], a["L0_ffn_sup_w"].reshape(SHARED, HIDDEN, D)], 0).transpose(2, 0, 1)
    down = _np.concatenate([a["L0_ffn_down_w"].transpose(2, 0, 1),
                            a["L0_ffn_sdown_w"].reshape(D, SHARED, HIDDEN).transpose(2, 1, 0)], 1)
    ffn = _np.stack([gate, up, down], 2)
    arrays = {
        "x": a["L0_attn_x"],
        "gamma": a["L0_attn_ln_gamma"].reshape(D, 1),
        "beta": a["L0_attn_ln_beta"].reshape(D, 1),
        "wqkv": wqkv,
        "wout": wo,
        "bout": _np.broadcast_to(a["L0_attn_b_out"], (P, D)),
        "rope": rope_tables(),
        "router_w": a["L0_ffn_router_w"].T,
        "router_b": _np.broadcast_to(a["L0_ffn_router_bias"], (P, EXPERTS)),
        "ffn_w": ffn,
    }
    arrays = {f"in_{k}": _np.ascontiguousarray(v) for k, v in arrays.items()}
    nc = _bacc.Bacc("TRN2", target_bir_lowering=False, num_devices=1)
    args = [nc.dram_tensor(k, v.shape, _mybir.dt.from_np(v.dtype), kind="ExternalInput").ap()
            for k, v in arrays.items()]
    out = nc.dram_tensor("out_0", (BATCH, SEQ, D), _mybir.dt.float32, kind="ExternalOutput").ap()
    layer_program(nc, *args, out)
    r = _run(nc, [arrays], core_ids=[0])
    return r.results[0]["out_0"]
```

```python
from contextlib import ExitStack

import numpy as np

import concourse.bass as bass
from concourse import mybir

F32 = mybir.dt.float32
F32R = mybir.dt.float32r
ALU = mybir.AluOpType
ACT = mybir.ActivationFunctionType
AX_X = mybir.AxisListType.X

P = 128
BATCH, SEQ, D = 4, 512, 128
HEADS, HEAD_DIM = 16, 64
TILES = SEQ // P
PAIRS = HEADS // 2
HEAD_SLOTS = BATCH * HEADS
EXPERTS, HIDDEN, TOP_K = 32, 128, 4
SHARED = 4
BLOCKS = EXPERTS + SHARED
ITEMS = BLOCKS * BATCH
EPS = 1e-5
HALF = HEAD_DIM // 2


def positive(eng, sem, value):
    if not isinstance(value, int) or value > 0:
        eng.wait_ge(sem, value)


def at_most(value, limit):
    return min(value, limit) if isinstance(value, int) else value


def run_slots(eng, slot, total, early, late):
    turns = total // 8
    for n in range(-early, 8):
        slot(n // 8, n % 8, lambda k, n=n: 0 <= n + k < total)
    with eng.Fori(1, turns - 1) as h:
        for r in range(8):
            slot(h, r, lambda k: True)
    for n in range(total - 8, total + late):
        slot(n // 8, n % 8, lambda k, n=n: 0 <= n + k < total)


def layer_program(nc, x, gamma, beta, wqkv, wout, bout, rope, router_w, router_b, ffn_w, out):
    with ExitStack() as ctx:
        def sb(name, shape, dt=F32):
            return ctx.enter_context(nc.sbuf_tensor(name, shape, dt))

        def sem(name):
            return ctx.enter_context(nc.semaphore(name))

        psum = ctx.enter_context(nc.psum_tensor("psum", [P, 8, 512], F32))

        ident = sb("ident", [P, P])
        gamma_c = sb("gamma_c", [P, 1])
        beta_c = sb("beta_c", [P, 1])
        eps_c = sb("eps_c", [P, 1])
        ones_c = sb("ones_c", [P, 1])
        bout_row = sb("bout_row", [P, D])
        rbias_row = sb("rbias_row", [P, EXPERTS])
        router_sb = sb("router_sb", [D, EXPERTS])
        rope_sb = sb("rope_sb", [P, 2, 2, SEQ])

        x_tok = sb("x_tok", [P, BATCH * TILES, D])
        normed_tok = sb("normed_tok", [P, BATCH * TILES, D])
        stats = sb("stats", [P, BATCH * TILES, 6])
        mean_var = sb("mean_var", [P, BATCH * TILES, 2])
        std = sb("std", [P, BATCH * TILES, 1])

        xT = sb("xT", [P, BATCH, SEQ])
        xT_hi = sb("xT_hi", [P, BATCH, SEQ], F32R)
        xT_lo = sb("xT_lo", [P, BATCH, SEQ], F32R)

        wqkv_raw = sb("wqkv_raw", [P, 3, P])
        wqkv_hi = sb("wqkv_hi", [P, 3, P], F32R)
        wqkv_lo = sb("wqkv_lo", [P, 3, P], F32R)
        wout_sb = sb("wout_sb", [P, PAIRS, 2, D])
        qk_flat = sb("qk_flat", [P, 2, SEQ])
        qk_swap = sb("qk_swap", [P, 2, SEQ])
        qk_hi = sb("qk_hi", [P, 2, 2, SEQ], F32R)
        qk_lo = sb("qk_lo", [P, 2, 2, SEQ], F32R)
        stacks = sb("stacks", [P, 2, 2, 3, SEQ], F32R)
        v_flat = sb("v_flat", [P, SEQ])
        v_parts = sb("v_parts", [P, 4, 2, TILES, P], F32R)
        neg_max = sb("neg_max", [P, 4, TILES])
        row_sum = sb("row_sum", [P, 4, TILES])
        inv_sum = sb("inv_sum", [P, 4, TILES])
        probs = sb("probs", [P, 4, TILES, SEQ])
        probsT_hi = sb("probsT_hi", [P, TILES, SEQ], F32R)
        probsT_lo = sb("probsT_lo", [P, TILES, SEQ], F32R)
        headT = sb("headT", [P, 2, SEQ])

        logits = sb("logits", [P, 16, EXPERTS])
        row_stat = sb("row_stat", [P, 4, 16])
        SENT = EXPERTS + 4
        scores_r = sb("scores_r", [P, 16, SENT])
        marked = sb("marked", [P, 16, SENT])
        top8 = sb("top8", [P, 16, 8])
        weights_tok = probs[:, 0, :, :].rearrange("p t (a e) -> p (t a) e", e=P)
        weightsT = sb("weightsT", [P, BATCH, SEQ], F32R)

        ffn_raw = sb("ffn_raw", [P, 2, 3, P])
        ffn_hi = sb("ffn_hi", [P, 2, 3, P], F32R)
        ffn_lo = sb("ffn_lo", [P, 2, 3, P], F32R)
        pick = sb("pick", [P, BLOCKS])
        pick_wide = sb("pick_wide", [P, 2, P], F32R)
        yT = probs[:, 3, :, :]
        silu = probs[:, 1, 0:2, :]
        hidden = probs[:, 1, 2:4, :]
        hidden_w = probs[:, 2, 0:2, :]
        hidden_hi = probsT_hi[:, 0:2, :]
        hidden_lo = probsT_lo[:, 0:2, :]

        x_in = [sem(f"x_in{b}") for b in range(BATCH)]
        consts_in = sem("consts_in")
        ident_step = sem("ident_step")
        eps_set = sem("eps_set")
        back_turned = sem("back_turned")
        summed = sem("summed")
        stats_done = sem("stats_done")
        var_done = sem("var_done")
        std_done = sem("std_done")
        rstd_done = sem("rstd_done")
        normed = sem("normed")
        norm_turned = sem("norm_turned")
        xT_done = sem("xT_done")
        xT_hi_done = sem("xT_hi_done")
        xT_lo_done = sem("xT_lo_done")
        resid_done = sem("resid_done")
        out_done = sem("out_done")
        wqkv_in = sem("wqkv_in")
        wout_in = sem("wout_in")
        wq_staged = [sem(f"wqkv_staged{m}") for m in range(3)]
        wq_step = sem("wq_step")
        q_projected, k_projected, v_projected = sem("q_projected"), sem("k_projected"), sem("v_projected")
        q_flat_done, k_flat_done, v_flat_done = sem("q_flat_done"), sem("k_flat_done"), sem("v_flat_done")
        swapped = [sem("q_swapped"), sem("k_swapped")]
        rope_step = sem("rope_step")
        turned_by = [sem("q_turned_by"), sem("k_turned_by")]
        qk_hi_done = [sem("q_hi_done"), sem("k_hi_done")]
        rotated = [sem("q_rotated"), sem("k_rotated")]
        stacked = [sem("stacked0"), sem("stacked1")]
        v_turned = sem("v_turned")
        v_hi_done, v_lo_done = sem("v_hi_done"), sem("v_lo_done")
        scored = sem("scored")
        maxed = sem("maxed")
        exped = sem("exped")
        inverted = sem("inverted")
        probs_turned = sem("probs_turned")
        probsT_hi_done, probsT_lo_done = sem("probsT_hi_done"), sem("probsT_lo_done")
        mixed = sem("mixed")
        headT_done = sem("headT_done")
        head_projected = sem("head_projected")
        y_added = sem("y_added")
        r_logits = sem("r_logits")
        r_step = sem("r_step")
        r_exp = sem("r_exp")
        r_sent = sem("r_sent")
        weights_done = sem("weights_done")
        weights_turned = sem("weights_turned")
        weightsT_copied = sem("weightsT_copied")
        weightsT_done = sem("weightsT_done")
        pick_step = sem("pick_step")
        ffn_in = [sem("ffn_in0"), sem("ffn_in1")]
        ffn_step = sem("ffn_step")
        ffn_staged = sem("ffn_staged")
        gated, upped, spread = sem("gated"), sem("upped"), sem("spread")
        silu_done = sem("silu_done")
        hidden_done = sem("hidden_done")
        hidden_w_done = sem("hidden_w_done")
        hidden_hi_done, hidden_lo_done = sem("hidden_hi_done"), sem("hidden_lo_done")
        downed = sem("downed")
        ffn_y_out = sem("ffn_y_out")

        x_dram = x.rearrange("b (t p) d -> p b t d", p=P)
        out_dram = out.rearrange("b (t p) d -> p b t d", p=P)
        CONSTS = 16 * 7

        block = ctx.enter_context(nc.Block())

        def tiles_of(b):
            return slice(TILES * b, TILES * (b + 1))

        @block.sync
        def _(sp):
            for b in range(BATCH):
                sp.dma_start(x_tok[:, tiles_of(b), :], x_dram[:, b, :, :]).then_inc(x_in[b], 16)
                if b == 0:
                    sp.dma_start(wqkv_raw[:], wqkv[:, 0, :, :]).then_inc(wqkv_in, 16)
                    sp.dma_start(wout_sb[:], wout).then_inc(wout_in, 16)
            sp.dma_start(gamma_c[:], gamma).then_inc(consts_in, 16)
            sp.dma_start(beta_c[:], beta).then_inc(consts_in, 16)
            sp.dma_start(rope_sb[:], rope).then_inc(consts_in, 16)
            sp.dma_start(bout_row[:], bout).then_inc(consts_in, 16)
            sp.dma_start(rbias_row[:], router_b).then_inc(consts_in, 16)
            sp.dma_start(router_sb[:], router_w).then_inc(consts_in, 16)
            sp.dma_start(ffn_raw[:], ffn_w[:, 0:2, :, :]).then_inc(consts_in, 16)

            def value(v):
                if not isinstance(v, int):
                    sp.compute_val(v)
                return v

            def wait_all(*waits):
                for s, v in [(s, value(v)) for s, v in waits]:
                    positive(sp, s, v)

            def swap(m, done, w):
                wait_all((done, w + 1), (rotated[m], w))
                for piece in range(4):
                    src = HALF * piece
                    dst = HALF * (piece ^ 1)
                    sp.dma_start(qk_swap[dst:dst + HALF, m, :], qk_flat[src:src + HALF, m, :])\
                        .then_inc(swapped[m], 16)

            def stack(w, buf):
                wait_all((rotated[0], w + 1), (rotated[1], w + 1), (scored, 8 * w - 8))
                top, low = slice(0, HEAD_DIM), slice(HEAD_DIM, P)
                for s in range(2):
                    rows = slice(HEAD_DIM * s, HEAD_DIM * (s + 1))
                    for dst, src in ((stacks[top, buf, s, 0:2, :], qk_hi[rows, buf, :, :]),
                                     (stacks[low, buf, s, 0:2, :], qk_lo[rows, buf, :, :]),
                                     (stacks[top, buf, s, 2, :], qk_lo[rows, buf, 1, :]),
                                     (stacks[low, buf, s, 2, :], qk_hi[rows, buf, 1, :])):
                        sp.dma_start(dst.bitcast(F32), src.bitcast(F32)).then_inc(stacked[buf], 16)

            def slot(h, r, live):
                if r % 2 == 1 and live(5):
                    swap(0, q_flat_done, 4 * h + (r + 5) // 2)
                if r % 2 == 0 and live(4):
                    swap(1, k_flat_done, 4 * h + (r + 4) // 2)
                if r % 2 == 0 and live(2):
                    w, buf = 4 * h + (r + 2) // 2, (r + 2) // 2 % 2
                    stack(w, buf)
                if r == 0 and live(8):
                    nxt = value(h + 1)
                    for m in range(3):
                        sp.wait_ge(wq_staged[m], nxt)
                    sp.dma_start(wqkv_raw[:], wqkv[:, bass.ds(nxt, 1), :, :].rearrange("p a m n -> p (a m) n"))\
                        .then_inc(wqkv_in, 16)
            run_slots(sp, slot, HEAD_SLOTS, 5, 4)

            for par in range(2):
                sp.wait_ge(ffn_staged, par + 1)
                sp.dma_start(ffn_raw[:, par, :, :], ffn_w[:, 2 + par, :, :]).then_inc(ffn_in[par], 16)
            with sp.Fori(1, BLOCKS // 2 - 1) as h:
                for par in range(2):
                    block_no, count = value(2 * h + (2 + par)), value(2 * h + (par + 1))
                    sp.wait_ge(ffn_staged, count)
                    sp.dma_start(ffn_raw[:, par, :, :],
                                 ffn_w[:, bass.ds(block_no, 1), :, :].rearrange("p a m n -> p (a m) n"))\
                        .then_inc(ffn_in[par], 16)

            for b in range(BATCH):
                sp.wait_ge(normed, 2 * BATCH + b + 1)
                sp.dma_start(out_dram[:, b, :, :], normed_tok[:, tiles_of(b), :]).then_inc(out_done, 16)
            sp.wait_ge(out_done, 16 * BATCH)

        @block.tensor
        def _(pe):
            def three(dst, w_hi, w_lo, m_hi, m_lo, start=True, stop=True):
                nc.tensor.matmul(dst, w_lo, m_hi, start=start, stop=False)
                nc.tensor.matmul(dst, w_hi, m_lo, start=False, stop=False)
                return nc.tensor.matmul(dst, w_hi, m_hi, start=False, stop=stop)

            def turn_normed(norm):
                for b in range(BATCH):
                    pe.wait_ge(normed, BATCH * norm + b + 1)
                    for i in range(TILES):
                        mm = nc.tensor.transpose(psum[:, b, i * P:(i + 1) * P], normed_tok[:, TILES * b + i, :], ident[:])
                    mm.then_inc(norm_turned, 1)

            def turn_back(b):
                for i in range(TILES):
                    mm = nc.tensor.transpose(psum[:, 4 + b, i * P:(i + 1) * P], yT[:, b, i * P:(i + 1) * P], ident[:])
                mm.then_inc(back_turned, 1)

            pe.wait_ge(ident_step, 2)
            turn_normed(0)
            pe.wait_ge(xT_lo_done, BATCH)

            def slot(h, r, live):
                t = 8 * h + r
                for q in range(TILES):
                    c = 4 * t + q
                    if live(-2):
                        if q == 0:
                            pe.wait_ge(exped, 4 * (t - 1))
                        positive(pe, probsT_lo_done, c - 8 - 1)
                        for i in range(TILES):
                            mm = nc.tensor.transpose(psum[:, 2 + q % 2, i * P:(i + 1) * P],
                                                     probs[:, (r - 2) % 4, i, q * P:(q + 1) * P], ident[:])
                        mm.then_inc(probs_turned, 1)
                    if live(0):
                        if q == 0 and r % 2 == 0:
                            pe.wait_ge(stacked[r // 2 % 2], 128 * (2 * h + r // 4 + 1))
                        positive(pe, exped, c - 1)
                        st = stacks[:, r // 2 % 2, r % 2]
                        lhs = st[:, 0, q * P:(q + 1) * P]
                        nc.tensor.matmul(psum[:, q % 2, :], lhs, st[:, 2, :], start=True, stop=False)
                        nc.tensor.matmul(psum[:, q % 2, :], lhs, st[:, 1, :], start=False, stop=True)\
                            .then_inc(scored, 1)
                    back = 2 if q >= 2 else 3
                    if live(-back):
                        j, rr = (q + 2) % 4, (r - back) % 8
                        pe.wait_ge(probsT_lo_done, c - 10 + 1)
                        if j == 0:
                            positive(pe, headT_done, t - back - 1)
                            pair = 4 * h + (r - back) // 2
                            pe.wait_ge(v_lo_done, pair + 1)
                        lhs = v_parts[:, rr // 2, rr % 2, j, :]
                        dst = psum[:, 4 + rr % 2, :]
                        nc.tensor.matmul(dst, lhs, probsT_lo[:, j, :], start=(j == 0), stop=False)
                        nc.tensor.matmul(dst, lhs, probsT_hi[:, j, :], start=False, stop=(j == 3))\
                            .then_inc(mixed, 1)
                    if r % 2 == 1 and live(5):
                        b = (r + 5) // 2 % 4
                        w = 4 * h + (r + 5) // 2
                        if q == 1:
                            positive(pe, v_lo_done, w - 1)
                            positive(pe, k_flat_done, w)
                            pe.wait_ge(wq_staged[0], h + 1 + (r + 5) // 8)
                            three(psum[:, 6, :], wqkv_hi[:, 0, :], wqkv_lo[:, 0, :], xT_hi[:, b, :],
                                  xT_lo[:, b, :]).then_inc(q_projected, 1)
                        if q == 3:
                            pe.wait_ge(q_flat_done, w + 1)
                            pe.wait_ge(wq_staged[1], h + 1 + (r + 5) // 8)
                            three(psum[:, 6, :], wqkv_hi[:, 1, :], wqkv_lo[:, 1, :], xT_hi[:, b, :],
                                  xT_lo[:, b, :]).then_inc(k_projected, 1)
                    if r % 2 == 0 and live(2):
                        b = (r + 2) // 2 % 4
                        w = 4 * h + (r + 2) // 2
                        if q == 1:
                            pe.wait_ge(k_flat_done, at_most(w + 2, PAIRS * BATCH))
                            pe.wait_ge(wq_staged[2], h + 1 + (r + 2) // 8)
                            three(psum[:, 6, :], wqkv_hi[:, 2, :], wqkv_lo[:, 2, :], xT_hi[:, b, :],
                                  xT_lo[:, b, :]).then_inc(v_projected, 1)
                        if q == 3:
                            pe.wait_ge(v_flat_done, w + 1)
                            for i in range(TILES):
                                mm = nc.tensor.transpose(psum[:, 6, i * P:(i + 1) * P],
                                                         v_flat[:, i * P:(i + 1) * P], ident[:])
                            mm.then_inc(v_turned, 1)
                    if q == 3 and live(-3):
                        s = (r - 3) % 2
                        if isinstance(t, int) and t == 3:
                            pe.wait_ge(wout_in, 16)
                        pe.wait_ge(headT_done, t - 3 + 1)
                        positive(pe, y_added, t - 3)
                        weights = wout_sb[:, bass.ds(h + (r - 3) // 8, 1), s, :].rearrange("p a d -> p (a d)")
                        for i in range(TILES):
                            mm = nc.tensor.matmul(psum[:, 7, i * P:(i + 1) * P], headT[:, s, i * P:(i + 1) * P],
                                                  weights, start=True, stop=True)
                        mm.then_inc(head_projected, 1)

            run_slots(pe, slot, HEAD_SLOTS, 5, 4)

            turn_normed(1)

            pe.wait_ge(y_added, HEAD_SLOTS)
            pe.wait_ge(xT_done, 2 * BATCH)
            for n in range(BATCH * TILES):
                mm = nc.tensor.matmul(psum[:, 7, n * EXPERTS:(n + 1) * EXPERTS],
                                      xT[:, n // TILES, (n % TILES) * P:(n % TILES + 1) * P], router_sb[:],
                                      start=True, stop=True)
            mm.then_inc(r_logits, 1)
            pe.wait_ge(weights_done, 1)
            pe.wait_ge(r_sent, 2)
            pe.wait_ge(xT_lo_done, 2 * BATCH)
            for b in range(BATCH):
                for i in range(TILES):
                    mm = nc.tensor.transpose(psum[:, b, i * P:(i + 1) * P], weights_tok[:, TILES * b + i, :],
                                             ident[:])
                mm.then_inc(weights_turned, 1)

            def ffn_slot(h, r, live):
                k, par, b = 8 * h + r, r // 4, r % 4
                if live(0):
                    if b == 0:
                        pe.wait_ge(ffn_staged, 2 * h + par + 1)
                    positive(pe, silu_done, k)
                    three(psum[:, 4, :], ffn_hi[:, par, 0, :], ffn_lo[:, par, 0, :], xT_hi[:, b, :],
                          xT_lo[:, b, :]).then_inc(gated, 1)
                    positive(pe, hidden_done, k)
                    three(psum[:, 5, :], ffn_hi[:, par, 1, :], ffn_lo[:, par, 1, :], xT_hi[:, b, :],
                          xT_lo[:, b, :]).then_inc(upped, 1)
                    if isinstance(k, int) and k < BATCH:
                        pe.wait_ge(weightsT_done, BATCH)
                    positive(pe, hidden_w_done, k)
                    nc.tensor.matmul(psum[:, 6, :], pick_wide[:, par, :], weightsT[:, b, :],
                                     start=True, stop=True).then_inc(spread, 1)
                if live(-2):
                    r2 = (r - 2) % 8
                    par2, b2 = r2 // 4, r2 % 4
                    first = isinstance(k, int) and k - 2 < BATCH
                    last = isinstance(k, int) and k - 2 >= ITEMS - BATCH
                    pe.wait_ge(hidden_lo_done, k - 2 + 1)
                    three(psum[:, b2, :], ffn_hi[:, par2, 2, :], ffn_lo[:, par2, 2, :], hidden_hi[:, r2 % 2, :],
                          hidden_lo[:, r2 % 2, :], start=first, stop=last).then_inc(downed, 1)

            run_slots(pe, ffn_slot, ITEMS, 0, 2)

            pe.wait_ge(hidden_w_done, ITEMS)
            for b in range(BATCH):
                pe.wait_ge(ffn_y_out, b + 1)
                turn_back(b)

        @block.scalar
        def _(act):
            def norm_std(norm):
                for b in range(BATCH):
                    act.wait_ge(var_done, BATCH * norm + b + 1)
                    if norm == 0 and b == 0:
                        act.wait_ge(eps_set, 1)
                    nc.scalar.activation(std[:, tiles_of(b), :], mean_var[:, tiles_of(b), 1:2], ACT.Sqrt,
                                         bias=eps_c[:, 0:1]).then_inc(std_done, 1)

            def high_parts(norm):
                for b in range(BATCH):
                    act.wait_ge(xT_done, BATCH * norm + b + 1)
                    nc.scalar.activation(xT_hi[:, b, :], xT[:, b, :], ACT.Copy).then_inc(xT_hi_done, 1)

            norm_std(0)
            high_parts(0)

            def slot(h, r, live):
                t = 8 * h + r
                for q in range(TILES):
                    c = 4 * t + q
                    if q == 2 and live(-3):
                        act.wait_ge(mixed, 4 * t - 8)
                        positive(act, head_projected, t - 3 - 1)
                        nc.scalar.activation(headT[:, (r - 3) % 2, :], psum[:, 4 + (r - 3) % 2, :], ACT.Copy)\
                            .then_inc(headT_done, 1)
                    if r % 2 == 1 and q == 2 and live(5):
                        w = 4 * h + (r + 5) // 2
                        act.wait_ge(q_projected, w + 1)
                        positive(act, rotated[0], w)
                        nc.scalar.activation(qk_flat[:, 0, :], psum[:, 6, :], ACT.Copy).then_inc(q_flat_done, 1)
                    if r % 2 == 0 and q == 0 and live(4):
                        w = 4 * h + (r + 4) // 2
                        act.wait_ge(k_projected, w + 1)
                        positive(act, rotated[1], w)
                        nc.scalar.activation(qk_flat[:, 1, :], psum[:, 6, :], ACT.Copy).then_inc(k_flat_done, 1)
                    if r % 2 == 0 and q == 2 and live(2):
                        w = 4 * h + (r + 2) // 2
                        act.wait_ge(v_projected, w + 1)
                        positive(act, v_turned, w)
                        nc.scalar.activation(v_flat[:], psum[:, 6, :], ACT.Copy).then_inc(v_flat_done, 1)
                    for m, when in ((0, r % 2 == 0 and q == 3 and live(4)), (1, r % 2 == 1 and q == 2 and live(3))):
                        if when:
                            w = 4 * h + (r + 4 - m) // 2
                            act.wait_ge(turned_by[m], w + 1)
                            buf = (r + 4 - m) // 2 % 2
                            positive(act, stacked[buf], 128 * (2 * h + (r + 4 - m) // 4))
                            nc.scalar.activation(qk_hi[:, buf, m, :], qk_flat[:, m, :], ACT.Copy)\
                                .then_inc(qk_hi_done[m], 1)
                    if r % 2 == 1 and q == 0 and live(1):
                        w, buf = 4 * h + (r + 1) // 2, (r + 1) // 2 % 4
                        act.wait_ge(v_turned, w + 1)
                        positive(act, mixed, 8 * w - 24)
                        nc.scalar.activation(
                            v_parts[:, buf, :, :, 0:HEAD_DIM].rearrange("p s i d -> p i s d"),
                            psum[:, 6, :].rearrange("p (i s d) -> p i s d", i=TILES, s=2),
                            ACT.Copy).then_inc(v_hi_done, 1)
                    if live(-2):
                        act.wait_ge(probs_turned, c - 8 + 1)
                        positive(act, mixed, c - 8 - 3)
                        nc.scalar.activation(probsT_hi[:, q, :], psum[:, 2 + q % 2, :], ACT.Copy)\
                            .then_inc(probsT_hi_done, 1)
                    if live(0):
                        act.wait_ge(maxed, c + 1)
                        if q == 0:
                            positive(act, probs_turned, 4 * t - 12)
                        nc.scalar.activation(probs[:, r % 4, q, :], psum[:, q % 2, :], ACT.Exp,
                                             bias=neg_max[:, r % 4, q:q + 1],
                                             accum_out=row_sum[:, r % 4, q:q + 1]).then_inc(exped, 1)

            run_slots(act, slot, HEAD_SLOTS, 5, 4)

            norm_std(1)
            for b in range(BATCH):
                act.wait_ge(norm_turned, BATCH + b + 1)
                nc.scalar.activation(xT[:, b, :], psum[:, b, :], ACT.Copy).then_inc(xT_done, 1)
            high_parts(1)
            act.wait_ge(r_step, 3)
            nc.scalar.activation(scores_r[:, :, 0:EXPERTS], logits[:], ACT.Exp).then_inc(r_exp, 1)
            for b in range(BATCH):
                act.wait_ge(weights_turned, b + 1)
                nc.scalar.activation(weightsT[:, b, :], psum[:, b, :], ACT.Copy).then_inc(weightsT_copied, 1)

            def ffn_slot(h, r, live):
                k = 8 * h + r
                if live(0):
                    act.wait_ge(gated, k + 1)
                    positive(act, hidden_done, k - 1)
                    nc.scalar.activation(silu[:, r % 2, :], psum[:, 4, :], ACT.Silu).then_inc(silu_done, 1)
                if live(-1):
                    act.wait_ge(hidden_w_done, k)
                    positive(act, downed, k - 2)
                    nc.scalar.activation(hidden_hi[:, (r - 1) % 2, :], hidden_w[:, (r - 1) % 2, :], ACT.Copy)\
                        .then_inc(hidden_hi_done, 1)

            run_slots(act, ffn_slot, ITEMS, 0, 1)

            for b in range(BATCH):
                act.wait_ge(downed, ITEMS - BATCH + b + 1)
                nc.scalar.activation(yT[:, b, :], psum[:, b, :], ACT.Copy).then_inc(ffn_y_out, 1)
            norm_std(2)

        @block.vector
        def _(dve):
            def norm_stats(norm, b):
                for n in range(TILES * b, TILES * (b + 1)):
                    ins = nc.vector.bn_stats(stats[:, n, :], x_tok[:, n, :])
                ins.then_inc(stats_done, 1)
                dve.wait_ge(stats_done, BATCH * norm + b + 1)
                for n in range(TILES * b, TILES * (b + 1)):
                    ins = nc.vector.bn_aggr(mean_var[:, n, :], stats[:, n, :])
                ins.then_inc(var_done, 1)

            def norm_apply(norm, b):
                dve.wait_ge(std_done, BATCH * norm + b + 1)
                nc.vector.reciprocal(std[:, tiles_of(b), :], std[:, tiles_of(b), :]).then_inc(rstd_done, 1)
                dve.wait_ge(rstd_done, BATCH * norm + b + 1)
                for n in range(TILES * b, TILES * (b + 1)):
                    ins = nc.vector.tensor_scalar(normed_tok[:, n, :], x_tok[:, n, :],
                                                  mean_var[:, n, 0:1], std[:, n, :], ALU.subtract, ALU.mult)
                ins.then_inc(normed, 1)

            def add_back(b):
                dve.wait_ge(back_turned, b + 1)
                nc.vector.tensor_tensor(x_tok[:, tiles_of(b), :],
                                        psum[:, 4 + b, :].rearrange("p (i d) -> p i d", i=TILES),
                                        normed_tok[:, tiles_of(b), :], ALU.add).then_inc(summed, 1)
                dve.wait_ge(summed, b + 1)

            nc.vector.memset(eps_c[:], EPS).then_inc(eps_set, 1)
            for b in range(BATCH):
                dve.wait_ge(x_in[b], 16)
                norm_stats(0, b)
            for b in range(BATCH):
                norm_apply(0, b)
            dve.wait_ge(consts_in, CONSTS)
            for b in range(BATCH):
                dve.wait_ge(norm_turned, b + 1)
                nc.vector.tensor_scalar(xT[:, b, :], psum[:, b, :], gamma_c[:, 0:1], beta_c[:, 0:1],
                                        ALU.mult, ALU.add).then_inc(xT_done, 1)
            for b in range(BATCH):
                dve.wait_ge(xT_hi_done, b + 1)
                nc.vector.tensor_tensor(xT_lo[:, b, :], xT[:, b, :], xT_hi[:, b, :].bitcast(F32),
                                        ALU.subtract).then_inc(xT_lo_done, 1)

            def slot(h, r, live):
                t = 8 * h + r
                for q in range(TILES):
                    c = 4 * t + q
                    if live(0):
                        dve.wait_ge(scored, c + 1)
                        if q == 0:
                            positive(dve, exped, 4 * t - 12)
                        nc.vector.tensor_reduce(neg_max[:, r % 4, q:q + 1], psum[:, q % 2, :], AX_X, ALU.max,
                                                negate=True).then_inc(maxed, 1)
                    if q == 0 and r % 2 == 1 and live(1):
                        w, buf = 4 * h + (r + 1) // 2, (r + 1) // 2 % 4
                        dve.wait_ge(v_hi_done, w + 1)
                        for s in range(2):
                            ins = nc.vector.tensor_tensor(
                                v_parts[:, buf, s, :, HEAD_DIM:P],
                                psum[:, 6, :].rearrange("p (i s d) -> p i s d", i=TILES, s=2)[:, :, s, :],
                                v_parts[:, buf, s, :, 0:HEAD_DIM].bitcast(F32), ALU.subtract)
                        ins.then_inc(v_lo_done, 1)
                    if live(-2):
                        dve.wait_ge(probsT_hi_done, c - 8 + 1)
                        nc.vector.tensor_tensor(probsT_lo[:, q, :], psum[:, 2 + q % 2, :],
                                                probsT_hi[:, q, :].bitcast(F32), ALU.subtract)\
                            .then_inc(probsT_lo_done, 1)
                    if q == 0 and live(-1):
                        dve.wait_ge(exped, 4 * t)
                        positive(dve, y_added, t - 4)
                        nc.vector.reciprocal(inv_sum[:, (r - 1) % 4, :], row_sum[:, (r - 1) % 4, :])\
                            .then_inc(inverted, 1)
                    if q == 1 and live(-4):
                        b = (r - 4) // 2 % 4
                        dve.wait_ge(head_projected, t - 3)
                        positive(dve, y_added, t - 4)
                        if isinstance(t, int) and t == 4:
                            dve.wait_ge(resid_done, 1)
                        for i in range(TILES):
                            n = TILES * b + i
                            ins = nc.vector.scalar_tensor_tensor(
                                x_tok[:, n, :], psum[:, 7, i * P:(i + 1) * P], inv_sum[:, (r - 4) % 4, i:i + 1],
                                x_tok[:, n, :], ALU.mult, ALU.add)
                        ins.then_inc(y_added, 1)

            run_slots(dve, slot, HEAD_SLOTS, 5, 4)

            dve.wait_ge(y_added, HEAD_SLOTS)
            for b in range(BATCH):
                norm_stats(1, b)
            for b in range(BATCH):
                norm_apply(1, b)
            for b in range(BATCH):
                dve.wait_ge(xT_hi_done, BATCH + b + 1)
                nc.vector.tensor_tensor(xT_lo[:, b, :], xT[:, b, :], xT_hi[:, b, :].bitcast(F32),
                                        ALU.subtract).then_inc(xT_lo_done, 1)

            step = [0]

            def chain(ins):
                step[0] += 1
                ins.then_inc(r_step, 1)
                dve.wait_ge(r_step, step[0])

            def wide(v):
                return v.rearrange("p (n a) -> p n a", a=1).broadcast_to([P, 16, EXPERTS])

            best, total = row_stat[:, 0, :], row_stat[:, 1, :]
            dve.wait_ge(r_logits, 1)
            chain(nc.vector.tensor_tensor(logits[:], psum[:, 7, :].rearrange("p (n e) -> p n e", e=EXPERTS),
                                          rbias_row[:].rearrange("p (a e) -> p a e", a=1)
                                          .broadcast_to([P, 16, EXPERTS]), ALU.add))
            chain(nc.vector.tensor_reduce(best, logits[:], AX_X, ALU.max))
            chain(nc.vector.tensor_tensor(logits[:], logits[:], wide(best), ALU.subtract))
            dve.wait_ge(r_exp, 1)
            dve.wait_ge(r_sent, 1)
            soft = scores_r[:, :, 0:EXPERTS]
            chain(nc.vector.tensor_reduce(total, soft, AX_X, ALU.add))
            chain(nc.vector.reciprocal(total, total))
            chain(nc.vector.tensor_tensor(soft, soft, wide(total), ALU.mult))
            for n in range(16):
                ins = nc.vector.max(top8[:, n, :], scores_r[:, n, 0:EXPERTS])
            chain(ins)
            chain(nc.vector.memset(top8[:, :, TOP_K:8], -1.0))
            for n in range(16):
                ins = nc.vector.match_replace(marked[:, n, :], top8[:, n, :], scores_r[:, n, :], -2.0)
            chain(ins)
            chosen = weights_tok[:, :, 0:EXPERTS]
            chain(nc.vector.scalar_tensor_tensor(chosen, marked[:, :, 0:EXPERTS], -2.0, soft,
                                                 ALU.is_equal, ALU.mult))
            chain(nc.vector.tensor_reduce(total, chosen, AX_X, ALU.add))
            chain(nc.vector.tensor_scalar(total, total, 1e-12, None, ALU.max))
            chain(nc.vector.reciprocal(total, total))
            chain(nc.vector.tensor_tensor(chosen, chosen, wide(total), ALU.mult))
            nc.vector.tensor_copy(weights_tok[:, :, EXPERTS:2 * EXPERTS], chosen).then_inc(weights_done, 1)
            lo_rows = slice(EXPERTS, 2 * EXPERTS)
            for b in range(BATCH):
                dve.wait_ge(weightsT_copied, b + 1)
                nc.vector.tensor_tensor(weightsT[lo_rows, b, :], psum[lo_rows, b, :],
                                        weightsT[lo_rows, b, :].bitcast(F32), ALU.subtract)\
                    .then_inc(weightsT_done, 1)

            def ffn_slot(h, r, live):
                k = 8 * h + r
                if live(0):
                    dve.wait_ge(silu_done, k + 1)
                    dve.wait_ge(upped, k + 1)
                    nc.vector.tensor_tensor(hidden[:, r % 2, :], psum[:, 5, :], silu[:, r % 2, :], ALU.mult)\
                        .then_inc(hidden_done, 1)
                if live(-1):
                    dve.wait_ge(hidden_hi_done, k)
                    nc.vector.tensor_tensor(hidden_lo[:, (r - 1) % 2, :], hidden_w[:, (r - 1) % 2, :],
                                            hidden_hi[:, (r - 1) % 2, :].bitcast(F32), ALU.subtract)\
                        .then_inc(hidden_lo_done, 1)
                if live(0):
                    dve.wait_ge(spread, k + 1)
                    dve.wait_ge(hidden_done, k + 1)
                    positive(dve, hidden_lo_done, k - 1)
                    nc.vector.tensor_tensor(hidden_w[:, r % 2, :], psum[:, 6, :], hidden[:, r % 2, :], ALU.mult)\
                        .then_inc(hidden_w_done, 1)

            run_slots(dve, ffn_slot, ITEMS, 0, 1)

            for b in range(BATCH):
                add_back(b)
                norm_stats(2, b)
            for b in range(BATCH):
                norm_apply(2, b)

        @block.gpsimd
        def _(pool):
            nc.gpsimd.memset(ident[:], 0.0).then_inc(ident_step, 1)
            pool.wait_ge(ident_step, 1)
            nc.gpsimd.affine_select(out=ident[:], in_=ident[:], compare_op=ALU.not_equal, fill=1.0, base=0,
                                    pattern=[[-1, P]], channel_multiplier=1).then_inc(ident_step, 1)
            picks = [0]

            def pick_chain(ins):
                picks[0] += 1
                ins.then_inc(pick_step, 1)
                pool.wait_ge(pick_step, picks[0])

            pick_chain(nc.gpsimd.memset(pick[:], 0.0))
            for first in (0, EXPERTS):
                pick_chain(nc.gpsimd.affine_select(out=pick[:, 0:EXPERTS], in_=pick[:, 0:EXPERTS],
                                                   compare_op=ALU.not_equal, fill=1.0, base=-first,
                                                   pattern=[[-1, EXPERTS]], channel_multiplier=1))
            pick_chain(nc.gpsimd.affine_select(out=pick[:, EXPERTS:BLOCKS], in_=pick[:, EXPERTS:BLOCKS],
                                               compare_op=ALU.not_equal, fill=1.0, base=-2 * EXPERTS,
                                               pattern=[[0, SHARED]], channel_multiplier=1))
            nc.gpsimd.memset(scores_r[:, :, EXPERTS:SENT], -1.0).then_inc(r_sent, 1)
            pick_chain(nc.gpsimd.memset(ones_c[:], 1.0))

            rope_n, wq_n, ffn_n = [0], [0], [0]

            def split(hi, lo, raw, step, base, beside=None):
                one = ones_c[:, 0:1]
                if len(raw.shape) == 3:
                    one = one.rearrange("p (a b) -> p a b", a=1)
                nc.gpsimd.tensor_tensor(hi, raw, one.broadcast_to(list(raw.shape)), ALU.mult).then_inc(step, 1)
                if beside:
                    beside()
                pool.wait_ge(step, base + 1)
                return nc.gpsimd.tensor_tensor(lo, raw, hi.bitcast(F32), ALU.subtract)

            def stage_qkv(m, n):
                pool.wait_ge(wqkv_in, 16 * n + 16)
                used = (q_projected, k_projected, v_projected)[m]
                positive(pool, used, 4 * n)
                split(wqkv_hi[:, m, :], wqkv_lo[:, m, :], wqkv_raw[:, m, :], wq_step, 3 * n + m)\
                    .then_inc(wq_staged[m], 1)

            def rotate(m, w):
                done = (q_flat_done, k_flat_done)[m]
                pool.wait_ge(done, w + 1)
                pool.wait_ge(swapped[m], 64 * w + 64)
                nc.gpsimd.tensor_tensor(qk_flat[:, m, :], qk_flat[:, m, :], rope_sb[:, m, 0, :], ALU.mult)
                nc.gpsimd.tensor_tensor(qk_swap[:, m, :], qk_swap[:, m, :], rope_sb[:, m, 1, :], ALU.mult)\
                    .then_inc(rope_step, 1)
                pool.wait_ge(rope_step, 2 * w + m + 1)
                nc.gpsimd.tensor_tensor(qk_flat[:, m, :], qk_flat[:, m, :], qk_swap[:, m, :], ALU.add)\
                    .then_inc(turned_by[m], 1)

            def low_parts(m, w, buf):
                pool.wait_ge(qk_hi_done[m], w + 1)
                nc.gpsimd.tensor_tensor(qk_lo[:, buf, m, :], qk_flat[:, m, :], qk_hi[:, buf, m, :].bitcast(F32),
                                        ALU.subtract).then_inc(rotated[m], 1)

            for m in range(3):
                stage_qkv(m, 0)
            pool.wait_ge(consts_in, CONSTS)
            pool.wait_ge(normed, BATCH)
            nc.gpsimd.tensor_tensor(x_tok[:], x_tok[:], bout_row[:].rearrange("p (a d) -> p a d", a=1)
                                    .broadcast_to([P, BATCH * TILES, D]), ALU.add).then_inc(resid_done, 1)

            def slot(h, r, live):
                t = 8 * h + r
                if r == 2 and live(6):
                    stage_qkv(0, h + 1)
                    stage_qkv(1, h + 1)
                if r % 2 == 0 and live(4):
                    w, buf = 4 * h + (r + 4) // 2, (r + 4) // 2 % 2
                    rotate(0, w)
                    rotate(1, w)
                    low_parts(0, w, buf)
                    low_parts(1, w, buf)
                if r == 5 and live(0) and live(3):
                    stage_qkv(2, h + 1)
            run_slots(pool, slot, HEAD_SLOTS, 5, 4)

            pool.wait_ge(probs_turned, 4 * HEAD_SLOTS)
            nc.gpsimd.memset(weights_tok[:, :, 2 * EXPERTS:P], 0.0).then_inc(pick_step, 1)
            pool.wait_ge(pick_step, picks[0] + 1)
            nc.gpsimd.memset(weights_tok[:, :, 2 * EXPERTS:2 * EXPERTS + 1], 1.0).then_inc(r_sent, 1)

            def stage_block(h, par):
                e = 2 * h + par
                if isinstance(h, int) and h == 0:
                    pool.wait_ge(consts_in, CONSTS)
                else:
                    pool.wait_ge(ffn_in[par], 16 * h)
                positive(pool, downed, 4 * e - 4)

                def widen():
                    nc.gpsimd.tensor_copy(pick_wide[:, par, :], pick[:, bass.ds(e, 1)].broadcast_to([P, P]))

                split(ffn_hi[:, par, :, :], ffn_lo[:, par, :, :], ffn_raw[:, par, :, :], ffn_step, e, widen)\
                    .then_inc(ffn_staged, 1)

            stage_block(0, 0)
            stage_block(0, 1)
            def ffn_slot(h, r, live):
                par = r // 4
                if r % 4 == 0 and live(4) and (not isinstance(h, int) or h > 0 or par == 1):
                    if par == 0:
                        stage_block(h, 1)
                    else:
                        stage_block(h + 1, 0)

            run_slots(pool, ffn_slot, ITEMS, 0, 0)


def rope_tables():
    inv_freq = (np.float32(1.0) / np.float32(10000.0) ** (np.arange(0, HEAD_DIM, 2, dtype=np.float32) / np.float32(HEAD_DIM)))
    ang = np.arange(SEQ, dtype=np.float32)[None, :] * inv_freq.astype(np.float32)[:, None]
    cos, sin = np.cos(ang), np.sin(ang)
    cos = np.concatenate([cos] * 4, 0)
    sin = np.concatenate([-sin, sin] * 2, 0)
    k = np.stack([cos, sin], 1)
    return np.ascontiguousarray(np.stack([k * np.float32(HEAD_DIM ** -0.5), k], 1).astype(np.float32))


def kernel(**inputs):
    import numpy as _np
    import concourse.bacc as _bacc
    from concourse import mybir as _mybir
    from concourse.bass_utils import run_bass_kernel_spmd as _run

    a = {k: _np.asarray(v) for k, v in inputs.items()}
    wqkv = a["L0_attn_w_qkv"].reshape(D, 3, PAIRS, P).transpose(0, 2, 1, 3)
    wo = a["L0_attn_w_out"].reshape(PAIRS, 2, HEAD_DIM, D).transpose(2, 0, 1, 3)
    wo = _np.concatenate([wo, wo], 0)
    gate = _np.concatenate([a["L0_ffn_gate_w"], a["L0_ffn_sgate_w"].reshape(SHARED, HIDDEN, D)], 0).transpose(2, 0, 1)
    up = _np.concatenate([a["L0_ffn_up_w"], a["L0_ffn_sup_w"].reshape(SHARED, HIDDEN, D)], 0).transpose(2, 0, 1)
    down = _np.concatenate([a["L0_ffn_down_w"].transpose(2, 0, 1),
                            a["L0_ffn_sdown_w"].reshape(D, SHARED, HIDDEN).transpose(2, 1, 0)], 1)
    ffn = _np.stack([gate, up, down], 2)
    arrays = {
        "x": a["L0_attn_x"],
        "gamma": a["L0_attn_ln_gamma"].reshape(D, 1),
        "beta": a["L0_attn_ln_beta"].reshape(D, 1),
        "wqkv": wqkv,
        "wout": wo,
        "bout": _np.broadcast_to(a["L0_attn_b_out"], (P, D)),
        "rope": rope_tables(),
        "router_w": a["L0_ffn_router_w"].T,
        "router_b": _np.broadcast_to(a["L0_ffn_router_bias"], (P, EXPERTS)),
        "ffn_w": ffn,
    }
    arrays = {f"in_{k}": _np.ascontiguousarray(v) for k, v in arrays.items()}
    nc = _bacc.Bacc("TRN2", target_bir_lowering=False, num_devices=1)
    args = [nc.dram_tensor(k, v.shape, _mybir.dt.from_np(v.dtype), kind="ExternalInput").ap()
            for k, v in arrays.items()]
    out = nc.dram_tensor("out_0", (BATCH, SEQ, D), _mybir.dt.float32, kind="ExternalOutput").ap()
    layer_program(nc, *args, out)
    r = _run(nc, [arrays], core_ids=[0])
    return r.results[0]["out_0"]
```

```python
from contextlib import ExitStack

import numpy as np

import concourse.bass as bass
from concourse import mybir

F32 = mybir.dt.float32
F32R = mybir.dt.float32r
ALU = mybir.AluOpType
ACT = mybir.ActivationFunctionType
AX_X = mybir.AxisListType.X

P = 128
BATCH, SEQ, D = 4, 512, 128
HEADS, HEAD_DIM = 16, 64
TILES = SEQ // P
PAIRS = HEADS // 2
HEAD_SLOTS = BATCH * HEADS
GROUPS = PAIRS // 2
EXPERTS, HIDDEN, TOP_K = 32, 128, 4
SHARED = 4
BLOCKS = EXPERTS + SHARED
ITEMS = BLOCKS * BATCH
PLAIN = SHARED * BATCH
ROUTER_ITEMS = PLAIN
EPS = 1e-5
HALF = HEAD_DIM // 2


def positive(eng, sem, value):
    if not isinstance(value, int) or value > 0:
        eng.wait_ge(sem, value)


def at_most(value, limit):
    return min(value, limit) if isinstance(value, int) else value


def run_slots(eng, slot, total, early, late, peeled=1, body=8):
    turns = total // body
    for n in range(-early, body * peeled):
        slot(n // body, n % body, lambda k, n=n: 0 <= n + k < total)
    with eng.Fori(peeled, turns - 1) as h:
        for r in range(body):
            slot(h, r, lambda k: True)
    for n in range(total - body, total + late):
        slot(n // body, n % body, lambda k, n=n: 0 <= n + k < total)


def layer_program(nc, x, gamma, beta, wqk, wv, wout, bout, rope, router_w, router_b, ffn_w, weight_store, out):
    with ExitStack() as ctx:
        def sb(name, shape, dt=F32):
            return ctx.enter_context(nc.sbuf_tensor(name, shape, dt))

        def sem(name):
            return ctx.enter_context(nc.semaphore(name))

        psum = ctx.enter_context(nc.psum_tensor("psum", [P, 8, 512], F32))

        ident = sb("ident", [P, P])
        gamma_c = sb("gamma_c", [P, 1])
        beta_c = sb("beta_c", [P, 1])
        eps_c = sb("eps_c", [P, 1])
        ones_c = sb("ones_c", [P, 1])
        bout_row = sb("bout_row", [P, D])
        rbias_row = sb("rbias_row", [P, EXPERTS])
        router_sb = sb("router_sb", [D, EXPERTS])
        rope_sb = sb("rope_sb", [P, 2, 2, SEQ])

        x_tok = sb("x_tok", [P, BATCH * TILES, D])
        normed_tok = sb("normed_tok", [P, BATCH * TILES, D])
        stats = sb("stats", [P, BATCH * TILES, 6])
        mean_var = sb("mean_var", [P, BATCH * TILES, 2])
        std = sb("std", [P, BATCH * TILES, 1])

        xT = sb("xT", [P, BATCH, SEQ])
        xT_hi = sb("xT_hi", [P, BATCH, SEQ], F32R)
        xT_lo = sb("xT_lo", [P, BATCH, SEQ], F32R)

        wqk_raw = sb("wqk_raw", [P, 2, P])
        wqk_hi = sb("wqk_hi", [P, 2, P], F32R)
        wqk_lo = sb("wqk_lo", [P, 2, P], F32R)
        wv_raw = sb("wv_raw", [P, 2 * P])
        wv_hi = sb("wv_hi", [P, 2 * P], F32R)
        wv_lo = sb("wv_lo", [P, 2 * P], F32R)
        wout_sb = sb("wout_sb", [P, PAIRS, 2, D])
        qk_flat = sb("qk_flat", [P, 2, 2, SEQ])
        qk_swap = sb("qk_swap", [P, 2, 2, SEQ])
        qk_hi = sb("qk_hi", [P, 2, 2, SEQ], F32R)
        qk_lo = sb("qk_lo", [P, 2, 2, SEQ], F32R)
        stacks = sb("stacks", [P, 2, 2, 3, SEQ], F32R)
        v_kept = normed_tok
        v_parts = sb("v_parts", [P, 4, 2, TILES, P], F32R)
        neg_max = sb("neg_max", [P, 4, TILES])
        row_sum = sb("row_sum", [P, 4, TILES])
        inv_sum = sb("inv_sum", [P, 4, TILES])
        probs = sb("probs", [P, 4, TILES, SEQ])
        probsT_hi = sb("probsT_hi", [P, TILES, SEQ], F32R)
        probsT_lo = sb("probsT_lo", [P, TILES, SEQ], F32R)
        headT = sb("headT", [P, 2, SEQ])

        logits = sb("logits", [P, 16, EXPERTS])
        row_stat = sb("row_stat", [P, 4, 16])
        SENT = EXPERTS + 4
        scores_r = sb("scores_r", [P, 16, SENT])
        marked = sb("marked", [P, 16, SENT])
        top8 = sb("top8", [P, 16, 8])
        weights_tok = sb("weights_tok", [P, BATCH * TILES, EXPERTS])
        weightsT = qk_flat[0:EXPERTS].rearrange("p a m n -> p (a m n)")

        ffn_raw = sb("ffn_raw", [P, 2, 3, P])
        ffn_hi = sb("ffn_hi", [P, 2, 3, P], F32R)
        ffn_lo = sb("ffn_lo", [P, 2, 3, P], F32R)
        weights_wide = (probs[:, 0, :, :], probs[:, 3, :, :])
        yT = probs[:, 3, :, :]
        silu = probs[:, 1, 0:2, :]
        hidden = probs[:, 1, 2:4, :]
        hidden_w = probs[:, 2, 0:2, :]
        hidden_hi = probsT_hi[:, 0:2, :]
        hidden_lo = probsT_lo[:, 0:2, :]

        x_in = [sem(f"x_in{b}") for b in range(BATCH)]
        norm_consts_in = sem("norm_consts_in")
        rope_in = sem("rope_in")
        late_consts_in = sem("late_consts_in")
        ident_step = sem("ident_step")
        eps_set = sem("eps_set")
        back_turned = sem("back_turned")
        summed = sem("summed")
        stats_done = sem("stats_done")
        var_done = sem("var_done")
        std_done = sem("std_done")
        rstd_done = sem("rstd_done")
        shift_done = sem("shift_done")
        normed = sem("normed")
        last_normed = sem("last_normed")
        norm_turned = sem("norm_turned")
        xT_done = sem("xT_done")
        xT_hi_done = sem("xT_hi_done")
        xT_lo_done = sem("xT_lo_done")
        resid_done = sem("resid_done")
        out_done = sem("out_done")
        wqk_in = sem("wqk_in")
        wv_in = sem("wv_in")
        wout_in = sem("wout_in")
        wq_staged = [sem("wq_staged"), sem("wk_staged")]
        wv_staged = sem("wv_staged")
        wv_step = sem("wv_step")
        wq_step = sem("wq_step")
        q_projected, k_projected = sem("q_projected"), sem("k_projected")
        v_projected = [sem("v_projected0"), sem("v_projected1")]
        q_flat_done, k_flat_done = sem("q_flat_done"), sem("k_flat_done")
        swapped = [[sem("q_swapped0"), sem("q_swapped1")], [sem("k_swapped0"), sem("k_swapped1")]]
        rope_step = [sem("q_rope_step"), sem("k_rope_step")]
        turned_by = [sem("q_turned_by"), sem("k_turned_by")]
        qk_hi_done = [sem("q_hi_done"), sem("k_hi_done")]
        rotated = [sem("q_rotated"), sem("k_rotated")]
        stacked = [sem("stacked0"), sem("stacked1")]
        v_keeping = sem("v_keeping")
        v_half_hi_done, v_half_lo_done = sem("v_half_hi_done"), sem("v_half_lo_done")
        v_hi_done, v_lo_done = sem("v_hi_done"), sem("v_lo_done")
        scored = sem("scored")
        maxed = sem("maxed")
        exped = sem("exped")
        inverted = sem("inverted")
        probs_turned = sem("probs_turned")
        probsT_hi_done, probsT_lo_done = sem("probsT_hi_done"), sem("probsT_lo_done")
        mixed = sem("mixed")
        headT_done = sem("headT_done")
        head_projected = sem("head_projected")
        y_added = sem("y_added")
        r_logits = sem("r_logits")
        r_step = sem("r_step")
        r_exp = sem("r_exp")
        r_sent = sem("r_sent")
        weights_done = sem("weights_done")
        weights_turned = sem("weights_turned")
        weightsT_copied = sem("weightsT_copied")
        weights_stored = sem("weights_stored")
        wide_in = [sem("wide_in0"), sem("wide_in1")]
        ffn_in = [sem("ffn_in0"), sem("ffn_in1")]
        ffn_step = sem("ffn_step")
        ffn_staged = sem("ffn_staged")
        gated, upped = sem("gated"), sem("upped")
        ones_set = sem("ones_set")
        silu_done = sem("silu_done")
        hidden_done = sem("hidden_done")
        hidden_w_done = sem("hidden_w_done")
        hidden_hi_done, hidden_lo_done = sem("hidden_hi_done"), sem("hidden_lo_done")
        plain_lo_done = sem("plain_lo_done")
        downed = sem("downed")
        ffn_y_out = sem("ffn_y_out")

        BACK_BANKS = (7, 4, 5, 6)

        x_dram = x.rearrange("b (t p) d -> p b t d", p=P)
        out_dram = out.rearrange("b (t p) d -> p b t d", p=P)
        LATE_CONSTS = 16 * 4

        block = ctx.enter_context(nc.Block())

        def wait_up_used(eng, k):
            if isinstance(k, int) and k < PLAIN:
                positive(eng, hidden_w_done, k + 1)
            else:
                eng.wait_ge(hidden_done, k + 1 - PLAIN)

        def by_pool(k):
            return isinstance(k, int) and k < ROUTER_ITEMS and k % 4 != 0

        def wait_low_part(eng, k):
            if by_pool(k):
                eng.wait_ge(plain_lo_done, k - k // 4)
            elif isinstance(k, int) and k < ROUTER_ITEMS:
                eng.wait_ge(hidden_lo_done, k // 4 + 1)
            else:
                eng.wait_ge(hidden_lo_done, k + 1 - ROUTER_ITEMS + ROUTER_ITEMS // 4)

        def rotate(eng, m, w, buf, before):
            done = (q_flat_done, k_flat_done)[m]
            eng.wait_ge(done, w + 1)
            eng.wait_ge(swapped[m][buf], 64 * before + 64)
            flat, swap = qk_flat[:, buf, m, :], qk_swap[:, buf, m, :]
            eng.tensor_tensor(flat, flat, rope_sb[:, m, 0, :], ALU.mult)
            eng.tensor_tensor(swap, swap, rope_sb[:, m, 1, :], ALU.mult)\
                .then_inc(rope_step[m], 1)
            eng.wait_ge(rope_step[m], w + 1)
            eng.tensor_tensor(flat, flat, swap, ALU.add).then_inc(turned_by[m], 1)
            eng.wait_ge(turned_by[m], w + 1)
            positive(eng, stacked[buf], 128 * before)
            eng.tensor_tensor(qk_hi[:, buf, m, :], flat, ones_c[:, 0:1].broadcast_to([P, SEQ]), ALU.mult)\
                .then_inc(qk_hi_done[m], 1)
            eng.wait_ge(qk_hi_done[m], w + 1)
            eng.tensor_tensor(qk_lo[:, buf, m, :], flat, qk_hi[:, buf, m, :].bitcast(F32), ALU.subtract)\
                .then_inc(rotated[m], 1)

        def tiles_of(b):
            return slice(TILES * b, TILES * (b + 1))

        @block.sync
        def _(sp):
            sp.dma_start(x_tok[:, tiles_of(0), :], x_dram[:, 0, :, :]).then_inc(x_in[0], 16)
            sp.dma_start(gamma_c[:], gamma).then_inc(norm_consts_in, 16)
            sp.dma_start(beta_c[:], beta).then_inc(norm_consts_in, 16)
            sp.dma_start(wqk_raw[:], wqk[:, 0, :, :]).then_inc(wqk_in, 16)
            sp.dma_start(rope_sb[:], rope).then_inc(rope_in, 16)
            sp.dma_start(wv_raw[:], wv[:, 0, :]).then_inc(wv_in, 16)
            sp.dma_start(bout_row[:], bout).then_inc(late_consts_in, 16)
            sp.dma_start(wout_sb[:], wout).then_inc(wout_in, 16)
            sp.dma_start(rbias_row[:], router_b).then_inc(late_consts_in, 16)
            sp.dma_start(router_sb[:], router_w).then_inc(late_consts_in, 16)
            sp.dma_start(ffn_raw[:], ffn_w[:, 0:2, :, :]).then_inc(late_consts_in, 16)

            def value(v):
                if not isinstance(v, int):
                    sp.compute_val(v)
                return v

            def wait_all(*waits):
                for s, v in [(s, value(v)) for s, v in waits]:
                    positive(sp, s, v)

            def swap(m, done, w, buf):
                wait_all((done, w + 1), (rotated[m], w - 1))
                for piece in range(4):
                    src = HALF * piece
                    dst = HALF * (piece ^ 1)
                    sp.dma_start(qk_swap[dst:dst + HALF, buf, m, :], qk_flat[src:src + HALF, buf, m, :])\
                        .then_inc(swapped[m][buf], 16)

            def stack(w, buf):
                wait_all((rotated[0], w + 1), (rotated[1], w + 1), (scored, 8 * w - 8))
                top, low = slice(0, HEAD_DIM), slice(HEAD_DIM, P)
                for s in range(2):
                    rows = slice(HEAD_DIM * s, HEAD_DIM * (s + 1))
                    for dst, src in ((stacks[top, buf, s, 0:2, :], qk_hi[rows, buf, :, :]),
                                     (stacks[low, buf, s, 0:2, :], qk_lo[rows, buf, :, :]),
                                     (stacks[top, buf, s, 2, :], qk_lo[rows, buf, 1, :]),
                                     (stacks[low, buf, s, 2, :], qk_hi[rows, buf, 1, :])):
                        sp.dma_start(dst.bitcast(F32), src.bitcast(F32)).then_inc(stacked[buf], 16)

            def slot(h, r, live):
                if r % 2 == 1 and live(5):
                    swap(0, q_flat_done, 8 * h + (r + 5) // 2, (r + 5) // 2 % 2)
                if r % 2 == 0 and live(4):
                    swap(1, k_flat_done, 8 * h + (r + 4) // 2, (r + 4) // 2 % 2)
                if r % 2 == 0 and live(2):
                    w, buf = 8 * h + (r + 2) // 2, (r + 2) // 2 % 2
                    stack(w, buf)
                if r % 8 == 0 and live(8):
                    nxt = value(2 * h + (r // 8 + 1))
                    for m in range(2):
                        sp.wait_ge(wq_staged[m], nxt)
                    sp.dma_start(wqk_raw[:], wqk[:, bass.ds(nxt, 1), :, :].rearrange("p a m n -> p (a m) n"))\
                        .then_inc(wqk_in, 16)
                if r == 0 and live(16):
                    nxt = value(h + 1)
                    sp.wait_ge(wv_staged, nxt)
                    sp.dma_start(wv_raw[:], wv[:, bass.ds(nxt, 1), :].rearrange("p a n -> p (a n)"))\
                        .then_inc(wv_in, 16)
            run_slots(sp, slot, HEAD_SLOTS, 5, 4, body=16)

            def load_block(h, par):
                block_no, count = value(2 * h + (2 + par)), value(2 * h + (par + 1))
                sp.wait_ge(ffn_staged, count)
                sp.dma_start(ffn_raw[:, par, :, :],
                             ffn_w[:, bass.ds(block_no, 1), :, :].rearrange("p a m n -> p (a m) n"))\
                    .then_inc(ffn_in[par], 16)

            def load_wide(h, par):
                expert = value(2 * h + (par - SHARED))
                used = value(8 * h + (4 * par - BATCH))
                if not isinstance(h, int) or h > 2:
                    sp.wait_ge(hidden_w_done, used)
                sp.dma_start(weights_wide[par].rearrange("p b n -> p (b n)"),
                             weight_store[bass.ds(expert, 1), :].broadcast_to([P, BATCH * SEQ]))\
                    .then_inc(wide_in[par], 16)

            for h in range(2):
                load_block(h, 0)
                load_block(h, 1)
            sp.wait_ge(weightsT_copied, BATCH)
            sp.dma_start(weight_store, weightsT[:]).then_inc(weights_stored, 16)
            sp.wait_ge(weights_stored, 16)
            for par in range(2):
                load_wide(2, par)
                load_block(2, par)
            with sp.Fori(3, BLOCKS // 2 - 1) as h:
                for par in range(2):
                    load_wide(h, par)
                    load_block(h, par)
            for par in range(2):
                load_wide(BLOCKS // 2 - 1, par)

            for b in range(BATCH):
                if b < BATCH - 1:
                    sp.wait_ge(normed, 2 * BATCH + b + 1)
                else:
                    sp.wait_ge(last_normed, 1)
                sp.dma_start(out_dram[:, b, :, :], normed_tok[:, tiles_of(b), :]).then_inc(out_done, 16)
            sp.wait_ge(out_done, 16 * BATCH)

        @block.tensor
        def _(pe):
            def three(dst, w_hi, w_lo, m_hi, m_lo, start=True, stop=True):
                nc.tensor.matmul(dst, w_lo, m_hi, start=start, stop=False)
                nc.tensor.matmul(dst, w_hi, m_lo, start=False, stop=False)
                return nc.tensor.matmul(dst, w_hi, m_hi, start=False, stop=stop)

            def turn_normed(norm, b):
                pe.wait_ge(normed, BATCH * norm + b + 1)
                for i in range(TILES):
                    mm = nc.tensor.transpose(psum[:, b, i * P:(i + 1) * P], normed_tok[:, TILES * b + i, :], ident[:])
                mm.then_inc(norm_turned, 1)

            def turn_back(b):
                pe.wait_ge(ffn_y_out, b + 1)
                for i in range(TILES):
                    mm = nc.tensor.transpose(psum[:, BACK_BANKS[b], i * P:(i + 1) * P], yT[:, b, i * P:(i + 1) * P], ident[:])
                mm.then_inc(back_turned, 1)

            pe.wait_ge(ident_step, 2)

            def slot(h, r, live):
                t = 16 * h + r
                first = isinstance(t, int) and t + 5 < 2 * BATCH
                if first and t + 5 < BATCH:
                    turn_normed(0, t + 5)
                if isinstance(t, int) and t == HEAD_SLOTS + 2:
                    turn_normed(1, 0)
                    turn_normed(1, 1)
                if isinstance(t, int) and t == HEAD_SLOTS + 3:
                    turn_normed(1, 2)
                for q in range(TILES):
                    c = 4 * t + q
                    if live(-2):
                        if q == 0:
                            pe.wait_ge(exped, 4 * (t - 1))
                        positive(pe, probsT_lo_done, c - 8 - 1)
                        for i in range(TILES):
                            mm = nc.tensor.transpose(psum[:, 2 + q % 2, i * P:(i + 1) * P],
                                                     probs[:, (r - 2) % 4, i, q * P:(q + 1) * P], ident[:])
                        mm.then_inc(probs_turned, 1)
                    if live(0):
                        if q == 0 and r % 2 == 0:
                            pe.wait_ge(stacked[r // 2 % 2], 128 * (4 * h + r // 4 + 1))
                        positive(pe, exped, c - 1)
                        st = stacks[:, r // 2 % 2, r % 2]
                        lhs = st[:, 0, q * P:(q + 1) * P]
                        nc.tensor.matmul(psum[:, q % 2, :], lhs, st[:, 2, :], start=True, stop=False)
                        nc.tensor.matmul(psum[:, q % 2, :], lhs, st[:, 1, :], start=False, stop=True)\
                            .then_inc(scored, 1)
                    back = 2 if q >= 2 else 3
                    if live(-back):
                        j, rr = (q + 2) % 4, (r - back) % 8
                        pe.wait_ge(probsT_lo_done, c - 10 + 1)
                        if j == 0:
                            positive(pe, headT_done, t - back - 1)
                            pair = 8 * h + (r - back) // 2
                            pe.wait_ge(v_lo_done, pair + 1)
                        lhs = v_parts[:, rr // 2, rr % 2, j, :]
                        dst = psum[:, 4 + rr % 2, :]
                        nc.tensor.matmul(dst, lhs, probsT_lo[:, j, :], start=(j == 0), stop=False)
                        nc.tensor.matmul(dst, lhs, probsT_hi[:, j, :], start=False, stop=(j == 3))\
                            .then_inc(mixed, 1)
                    if r % 2 == 1 and live(5):
                        b = (r + 5) // 2 % 4
                        w = 8 * h + (r + 5) // 2
                        if q == 1 and first:
                            pe.wait_ge(xT_lo_done, b + 1)
                        if q == 1:
                            positive(pe, v_lo_done, w - 1)
                            positive(pe, k_flat_done, w)
                            pe.wait_ge(wq_staged[0], 2 * h + 1 + (r + 5) // 8)
                            three(psum[:, 6, :], wqk_hi[:, 0, :], wqk_lo[:, 0, :], xT_hi[:, b, :],
                                  xT_lo[:, b, :]).then_inc(q_projected, 1)
                        if q == 3:
                            pe.wait_ge(q_flat_done, w + 1)
                            pe.wait_ge(wq_staged[1], 2 * h + 1 + (r + 5) // 8)
                            three(psum[:, 6, :], wqk_hi[:, 1, :], wqk_lo[:, 1, :], xT_hi[:, b, :],
                                  xT_lo[:, b, :]).then_inc(k_projected, 1)
                    if r % 2 == 0 and (r + 2) // 2 % 8 < BATCH and live(2) and q % 2 == 1:
                        b, half = (r + 2) // 2 % 4, q // 2
                        w = 8 * h + (r + 2) // 2
                        if half == 0:
                            pe.wait_ge(k_flat_done, at_most(w + 2, PAIRS * BATCH))
                            pe.wait_ge(wv_staged, h + 1 + (r + 2) // 16)
                        else:
                            pe.wait_ge(v_half_lo_done, 4 * (h + (r + 2) // 16) + b + 1)
                        for i in range(2):
                            tile = slice((2 * half + i) * P, (2 * half + i + 1) * P)
                            mm = three(psum[:, 6, i * 2 * P:(i + 1) * 2 * P], xT_hi[:, b, tile], xT_lo[:, b, tile],
                                       wv_hi[:], wv_lo[:])
                        mm.then_inc(v_projected[half], 1)
                    if q == 3 and live(-3):
                        s = (r - 3) % 2
                        if isinstance(t, int) and t == 3:
                            pe.wait_ge(wout_in, 16)
                        pe.wait_ge(headT_done, t - 3 + 1)
                        positive(pe, y_added, t - 3)
                        weights = wout_sb[:, bass.ds(2 * h + (r - 3) // 8, 1), s, :].rearrange("p a d -> p (a d)")
                        for i in range(TILES):
                            mm = nc.tensor.matmul(psum[:, 7, i * P:(i + 1) * P], headT[:, s, i * P:(i + 1) * P],
                                                  weights, start=True, stop=True)
                        mm.then_inc(head_projected, 1)

            run_slots(pe, slot, HEAD_SLOTS, 5, 4, body=16)

            def router_logits():
                pe.wait_ge(y_added, HEAD_SLOTS)
                pe.wait_ge(xT_done, 2 * BATCH)
                pe.wait_ge(late_consts_in, LATE_CONSTS)
                for n in range(BATCH * TILES):
                    mm = nc.tensor.matmul(psum[:, 7, n * EXPERTS:(n + 1) * EXPERTS],
                                          xT[:, n // TILES, (n % TILES) * P:(n % TILES + 1) * P], router_sb[:],
                                          start=True, stop=True)
                mm.then_inc(r_logits, 1)

            def turn_weights(b):
                if b == 0:
                    pe.wait_ge(weights_done, 1)
                positive(pe, weightsT_copied, b - 1)
                for i in range(TILES):
                    mm = nc.tensor.transpose(psum[0:EXPERTS, 7 - b % 2, i * P:(i + 1) * P],
                                             weights_tok[:, TILES * b + i, :], ident[:])
                mm.then_inc(weights_turned, 1)

            pe.wait_ge(headT_done, HEAD_SLOTS)

            def ffn_slot(h, r, live):
                k, par, b = 8 * h + r, r // 4, r % 4
                plain = isinstance(k, int) and k < PLAIN
                if isinstance(k, int) and k == 2:
                    turn_normed(1, BATCH - 1)
                if live(0):
                    if b == 0:
                        pe.wait_ge(ffn_staged, 2 * h + par + 1)
                    if isinstance(k, int) and k < BATCH:
                        pe.wait_ge(xT_lo_done, BATCH + b + 1)
                    positive(pe, silu_done, k)
                    three(psum[:, 4, :], ffn_hi[:, par, 0, :], ffn_lo[:, par, 0, :], xT_hi[:, b, :],
                          xT_lo[:, b, :]).then_inc(gated, 1)
                    up_bank = 5 if plain else 5 + r % 2
                    if plain:
                        wait_up_used(pe, k - 1)
                    else:
                        wait_up_used(pe, k - 2 if not isinstance(k, int) or k > PLAIN else k - 1)
                        if isinstance(k, int) and k == PLAIN + 1:
                            pe.wait_ge(weightsT_copied, BATCH)
                    three(psum[:, up_bank, :], ffn_hi[:, par, 1, :], ffn_lo[:, par, 1, :], xT_hi[:, b, :],
                          xT_lo[:, b, :]).then_inc(upped, 1)
                if live(-2):
                    r2 = (r - 2) % 8
                    par2, b2 = r2 // 4, r2 % 4
                    first = isinstance(k, int) and k - 2 < BATCH
                    last = isinstance(k, int) and k - 2 >= ITEMS - BATCH
                    wait_low_part(pe, k - 2)
                    three(psum[:, b2, :], ffn_hi[:, par2, 2, :], ffn_lo[:, par2, 2, :], hidden_hi[:, r2 % 2, :],
                          hidden_lo[:, r2 % 2, :], start=first, stop=last).then_inc(downed, 1)
                if isinstance(k, int) and k == ITEMS:
                    turn_back(0)
                if plain:
                    if k == 4:
                        router_logits()
                    if k == 12:
                        turn_weights(0)
                        turn_weights(1)
                    if k == 13:
                        turn_weights(2)
                        turn_weights(3)

            run_slots(pe, ffn_slot, ITEMS, 0, 2, peeled=3)

            pe.wait_ge(hidden_w_done, ITEMS)
            for b in range(1, BATCH):
                turn_back(b)

        @block.scalar
        def _(act):
            def norm_std(norm, b):
                act.wait_ge(var_done, BATCH * norm + b + 1)
                if norm == 0 and b == 0:
                    act.wait_ge(eps_set, 1)
                nc.scalar.activation(std[:, tiles_of(b), :], mean_var[:, tiles_of(b), 1:2], ACT.Sqrt,
                                     bias=eps_c[:, 0:1]).then_inc(std_done, 1)

            def high_part(norm, b):
                act.wait_ge(xT_done, BATCH * norm + b + 1)
                nc.scalar.activation(xT_hi[:, b, :], xT[:, b, :], ACT.Copy).then_inc(xT_hi_done, 1)

            def take_turned(b):
                act.wait_ge(norm_turned, BATCH + b + 1)
                nc.scalar.activation(xT[:, b, :], psum[:, b, :], ACT.Copy).then_inc(xT_done, 1)
                high_part(1, b)

            def keep_v(g, b, half):
                act.wait_ge(v_projected[half], 4 * g + b + 1)
                tiles = slice(2 * half, 2 * half + 2)
                v = psum[:, 6, :].rearrange("p (i o s d) -> p i o s d", i=2, o=2, s=2)
                if half == 0:
                    positive(act, v_lo_done, 8 * g + b - 3)
                    positive(act, mixed, 64 * g + 8 * b - 24)
                nc.scalar.activation(v_kept[:, TILES * b + 2 * half:TILES * b + 2 * half + 2, :]
                                     .rearrange("p i (s d) -> p i s d", s=2), v[:, :, 1, :, :], ACT.Copy)\
                    .then_inc(v_keeping, 1)
                nc.scalar.activation(v_parts[:, b, :, tiles, 0:HEAD_DIM].rearrange("p s i d -> p i s d"),
                                     v[:, :, 0, :, :], ACT.Copy).then_inc((v_half_hi_done, v_hi_done)[half], 1)

            def take_y(b):
                act.wait_ge(downed, ITEMS - BATCH + b + 1)
                nc.scalar.activation(yT[:, b, :], psum[:, b, :], ACT.Copy).then_inc(ffn_y_out, 1)

            def last_norm(b):
                act.wait_ge(shift_done, b + 1)
                for n in range(TILES * b, TILES * (b + 1)):
                    ins = nc.scalar.activation(normed_tok[:, n, :], x_tok[:, n, :], ACT.Identity,
                                               bias=mean_var[:, n, 0:1], scale=std[:, n, :])
                ins.then_inc(normed, 1)

            for b in range(1, BATCH):
                act.dma_start(x_tok[:, tiles_of(b), :], x_dram[:, b, :, :]).then_inc(x_in[b], 16)
            norm_std(0, 0)
            norm_std(0, 1)
            high_part(0, 0)

            def slot(h, r, live):
                t = 16 * h + r
                for q in range(TILES):
                    c = 4 * t + q
                    if q == 2 and live(-3):
                        act.wait_ge(mixed, 4 * t - 8)
                        positive(act, head_projected, t - 3 - 1)
                        nc.scalar.activation(headT[:, (r - 3) % 2, :], psum[:, 4 + (r - 3) % 2, :], ACT.Copy)\
                            .then_inc(headT_done, 1)
                    if r % 2 == 1 and q == 2 and live(5):
                        w = 8 * h + (r + 5) // 2
                        act.wait_ge(q_projected, w + 1)
                        positive(act, rotated[0], w - 1)
                        nc.scalar.activation(qk_flat[:, (r + 5) // 2 % 2, 0, :], psum[:, 6, :], ACT.Copy).then_inc(q_flat_done, 1)
                    if r % 2 == 0 and q == 0 and live(4):
                        w = 8 * h + (r + 4) // 2
                        act.wait_ge(k_projected, w + 1)
                        positive(act, rotated[1], w - 1)
                        nc.scalar.activation(qk_flat[:, (r + 4) // 2 % 2, 1, :], psum[:, 6, :], ACT.Copy).then_inc(k_flat_done, 1)
                    if isinstance(t, int) and (t, q) == (-4, 1):
                        high_part(0, 1)
                    if r % 2 == 0 and (r + 2) // 2 % 8 < BATCH and q == 2 and live(2):
                        keep_v(h + (r + 2) // 16, (r + 2) // 2 % 4, 0)
                    if r % 2 == 1 and q == 0 and live(1):
                        g, b = h + (r + 1) // 16, (r + 1) // 2 % 4
                        if (r + 1) // 2 % 8 < BATCH:
                            keep_v(g, b, 1)
                        else:
                            act.wait_ge(v_keeping, 8 * g + 2 * b + 2)
                            act.wait_ge(mixed, 64 * g + 8 * b + 8)
                            nc.scalar.activation(v_parts[:, b, :, :, 0:HEAD_DIM].rearrange("p s i d -> p i s d"),
                                                 v_kept[:, tiles_of(b), :].rearrange("p i (s d) -> p i s d", s=2),
                                                 ACT.Copy).then_inc(v_hi_done, 1)
                    if live(-2):
                        act.wait_ge(probs_turned, c - 8 + 1)
                        positive(act, mixed, c - 8 - 3)
                        nc.scalar.activation(probsT_hi[:, q, :], psum[:, 2 + q % 2, :], ACT.Copy)\
                            .then_inc(probsT_hi_done, 1)
                    if live(0):
                        act.wait_ge(maxed, c + 1)
                        if q == 0:
                            positive(act, probs_turned, 4 * t - 12)
                        nc.scalar.activation(probs[:, r % 4, q, :], psum[:, q % 2, :], ACT.Exp,
                                             bias=neg_max[:, r % 4, q:q + 1],
                                             accum_out=row_sum[:, r % 4, q:q + 1]).then_inc(exped, 1)
                if isinstance(t, int):
                    if t == -5:
                        norm_std(0, 2)
                        norm_std(0, 3)
                    if t in (-3, -2):
                        high_part(0, t + 5)
                    if t == HEAD_SLOTS - 1:
                        norm_std(1, 0)
                        norm_std(1, 1)
                    if t == HEAD_SLOTS + 1:
                        norm_std(1, 2)
                    if t == HEAD_SLOTS + 2:
                        take_turned(0)
                        take_turned(1)
                    if t == HEAD_SLOTS + 3:
                        take_turned(2)

            run_slots(act, slot, HEAD_SLOTS, 5, 4, body=16)

            norm_std(1, 3)

            def ffn_slot(h, r, live):
                k = 8 * h + r
                if live(0):
                    act.wait_ge(gated, k + 1)
                    wait_up_used(act, k - 2)
                    nc.scalar.activation(silu[:, r % 2, :], psum[:, 4, :], ACT.Silu).then_inc(silu_done, 1)
                if live(-1):
                    act.wait_ge(hidden_w_done, k)
                    positive(act, downed, k - 2)
                    nc.scalar.activation(hidden_hi[:, (r - 1) % 2, :], hidden_w[:, (r - 1) % 2, :], ACT.Copy)\
                        .then_inc(hidden_hi_done, 1)
                if isinstance(k, int):
                    if k == ITEMS - 1:
                        take_y(0)
                    if k == 1:
                        take_turned(3)
                    if k == 6:
                        act.wait_ge(r_step, 3)
                        act.wait_ge(r_sent, 1)
                        nc.scalar.activation(scores_r[:, :, 0:EXPERTS], logits[:], ACT.Exp).then_inc(r_exp, 1)
                    for b in {12: (0, 1), 13: (2, 3)}.get(k, ()):
                        act.wait_ge(weights_turned, b + 1)
                        nc.scalar.activation(weightsT[:, b * SEQ:(b + 1) * SEQ], psum[0:EXPERTS, 7 - b % 2, :], ACT.Copy)\
                            .then_inc(weightsT_copied, 1)

            run_slots(act, ffn_slot, ITEMS, 0, 1, peeled=3)

            for b in range(1, BATCH):
                take_y(b)
            norm_std(2, 0)
            for b in range(1, BATCH):
                norm_std(2, b)
                last_norm(b - 1)

        @block.vector
        def _(dve):
            def norm_stats(norm, b):
                for n in range(TILES * b, TILES * (b + 1)):
                    ins = nc.vector.bn_stats(stats[:, n, :], x_tok[:, n, :])
                ins.then_inc(stats_done, 1)
                dve.wait_ge(stats_done, BATCH * norm + b + 1)
                for n in range(TILES * b, TILES * (b + 1)):
                    ins = nc.vector.bn_aggr(mean_var[:, n, :], stats[:, n, :])
                ins.then_inc(var_done, 1)

            def norm_apply(norm, b, done=normed):
                dve.wait_ge(std_done, BATCH * norm + b + 1)
                nc.vector.reciprocal(std[:, tiles_of(b), :], std[:, tiles_of(b), :]).then_inc(rstd_done, 1)
                dve.wait_ge(rstd_done, BATCH * norm + b + 1)
                for n in range(TILES * b, TILES * (b + 1)):
                    ins = nc.vector.tensor_scalar(normed_tok[:, n, :], x_tok[:, n, :],
                                                  mean_var[:, n, 0:1], std[:, n, :], ALU.subtract, ALU.mult)
                ins.then_inc(done, 1)

            def add_back(b):
                dve.wait_ge(back_turned, b + 1)
                nc.vector.tensor_tensor(x_tok[:, tiles_of(b), :],
                                        psum[:, BACK_BANKS[b], :].rearrange("p (i d) -> p i d", i=TILES),
                                        normed_tok[:, tiles_of(b), :], ALU.add).then_inc(summed, 1)
                dve.wait_ge(summed, b + 1)

            nc.vector.memset(eps_c[:], EPS).then_inc(eps_set, 1)

            def first_stats(b):
                dve.wait_ge(x_in[b], 16)
                norm_stats(0, b)

            def scale_turned(b):
                if b == 0:
                    dve.wait_ge(norm_consts_in, 32)
                dve.wait_ge(norm_turned, b + 1)
                nc.vector.tensor_scalar(xT[:, b, :], psum[:, b, :], gamma_c[:, 0:1], beta_c[:, 0:1],
                                        ALU.mult, ALU.add).then_inc(xT_done, 1)

            def low_part(norm, b):
                dve.wait_ge(xT_hi_done, BATCH * norm + b + 1)
                nc.vector.tensor_tensor(xT_lo[:, b, :], xT[:, b, :], xT_hi[:, b, :].bitcast(F32),
                                        ALU.subtract).then_inc(xT_lo_done, 1)

            first_stats(0)
            norm_apply(0, 0)
            first_stats(1)
            scale_turned(0)
            norm_apply(0, 1)
            low_part(0, 0)
            first_stats(2)
            first_stats(3)
            norm_apply(0, 2)
            norm_apply(0, 3)
            def split_v(b, half):
                tiles = slice(2 * half, 2 * half + 2)
                v = psum[:, 6, :].rearrange("p (i o s d) -> p i o s d", i=2, o=2, s=2)
                return nc.vector.tensor_tensor(
                    v_parts[:, b, :, tiles, HEAD_DIM:P].rearrange("p s i d -> p i s d"), v[:, :, 0, :, :],
                    v_parts[:, b, :, tiles, 0:HEAD_DIM].rearrange("p s i d -> p i s d").bitcast(F32), ALU.subtract)

            dve.wait_ge(rope_in, 16)
            dve.wait_ge(ones_set, 1)

            def slot(h, r, live):
                t = 16 * h + r
                if isinstance(t, int) and t == -4:
                    scale_turned(1)
                    low_part(0, 1)
                    rotate(dve, 0, 0, 0, 0)
                    scale_turned(2)
                    rotate(dve, 1, 0, 0, 0)
                    low_part(0, 2)
                if isinstance(t, int) and t == -2:
                    scale_turned(3)
                if isinstance(t, int) and t == HEAD_SLOTS + 3:
                    low_part(1, 0)
                    low_part(1, 1)
                for q in range(TILES):
                    c = 4 * t + q
                    if live(0):
                        dve.wait_ge(scored, c + 1)
                        if q == 0:
                            positive(dve, exped, 4 * t - 12)
                        nc.vector.tensor_reduce(neg_max[:, r % 4, q:q + 1], psum[:, q % 2, :], AX_X, ALU.max,
                                                negate=True).then_inc(maxed, 1)
                    if q == 2 and r % 2 == 0 and (r + 2) // 2 % 8 < BATCH and live(2):
                        g, b = h + (r + 2) // 16, (r + 2) // 2 % 4
                        dve.wait_ge(v_half_hi_done, 4 * g + b + 1)
                        split_v(b, 0).then_inc(v_half_lo_done, 1)
                        if isinstance(t, int) and t == -2:
                            low_part(0, 3)
                    if q == 0 and r % 2 == 1 and live(1):
                        w, b = 8 * h + (r + 1) // 2, (r + 1) // 2 % 4
                        dve.wait_ge(v_hi_done, w + 1)
                        if (r + 1) // 2 % 8 < BATCH:
                            split_v(b, 1).then_inc(v_lo_done, 1)
                        else:
                            nc.vector.tensor_tensor(
                                v_parts[:, b, :, :, HEAD_DIM:P].rearrange("p s i d -> p i s d"),
                                v_kept[:, tiles_of(b), :].rearrange("p i (s d) -> p i s d", s=2),
                                v_parts[:, b, :, :, 0:HEAD_DIM].rearrange("p s i d -> p i s d").bitcast(F32),
                                ALU.subtract).then_inc(v_lo_done, 1)
                        if isinstance(t, int) and t == -1:
                            rotate(dve, 0, 1, 1, 0)
                    if live(-2):
                        dve.wait_ge(probsT_hi_done, c - 8 + 1)
                        nc.vector.tensor_tensor(probsT_lo[:, q, :], psum[:, 2 + q % 2, :],
                                                probsT_hi[:, q, :].bitcast(F32), ALU.subtract)\
                            .then_inc(probsT_lo_done, 1)
                    if q == 0 and live(-1):
                        dve.wait_ge(exped, 4 * t)
                        positive(dve, y_added, t - 4)
                        nc.vector.reciprocal(inv_sum[:, (r - 1) % 4, :], row_sum[:, (r - 1) % 4, :])\
                            .then_inc(inverted, 1)
                    if q == 1 and live(-4):
                        b = (r - 4) // 2 % 4
                        dve.wait_ge(head_projected, t - 3)
                        positive(dve, y_added, t - 4)
                        if isinstance(t, int) and t == 4:
                            dve.wait_ge(resid_done, 1)
                        for i in range(TILES):
                            n = TILES * b + i
                            ins = nc.vector.scalar_tensor_tensor(
                                x_tok[:, n, :], psum[:, 7, i * P:(i + 1) * P], inv_sum[:, (r - 4) % 4, i:i + 1],
                                x_tok[:, n, :], ALU.mult, ALU.add)
                        ins.then_inc(y_added, 1)
                if isinstance(t, int):
                    for b in {HEAD_SLOTS - 3: (0,), HEAD_SLOTS - 1: (1,), HEAD_SLOTS + 1: (2,),
                              HEAD_SLOTS + 3: (3,)}.get(t, ()):
                        dve.wait_ge(y_added, HEAD_SLOTS - 6 + 2 * b)
                        norm_stats(1, b)
                    if t == HEAD_SLOTS:
                        norm_apply(1, 0)
                        norm_apply(1, 1)
                    if t == HEAD_SLOTS + 2:
                        norm_apply(1, 2)
                    if t == HEAD_SLOTS + 3:
                        low_part(1, 2)

            run_slots(dve, slot, HEAD_SLOTS, 5, 4, body=16)

            norm_apply(1, 3)

            step = [0]

            def chain(ins):
                step[0] += 1
                ins.then_inc(r_step, 1)
                dve.wait_ge(r_step, step[0])

            def wide(v):
                return v.rearrange("p (n a) -> p n a", a=1).broadcast_to([P, 16, EXPERTS])

            best, total = row_stat[:, 0, :], row_stat[:, 1, :]
            soft = scores_r[:, :, 0:EXPERTS]
            chosen = weights_tok[:]

            def router(k):
                if k == 5:
                    dve.wait_ge(late_consts_in, LATE_CONSTS)
                    dve.wait_ge(r_logits, 1)
                    chain(nc.vector.tensor_tensor(logits[:], psum[:, 7, :].rearrange("p (n e) -> p n e", e=EXPERTS),
                                                  rbias_row[:].rearrange("p (a e) -> p a e", a=1)
                                                  .broadcast_to([P, 16, EXPERTS]), ALU.add))
                    chain(nc.vector.tensor_reduce(best, logits[:], AX_X, ALU.max))
                if k == 6:
                    chain(nc.vector.tensor_tensor(logits[:], logits[:], wide(best), ALU.subtract))
                if k == 7:
                    dve.wait_ge(r_exp, 1)
                    chain(nc.vector.tensor_reduce(total, soft, AX_X, ALU.add))
                    chain(nc.vector.reciprocal(total, total))
                    chain(nc.vector.tensor_tensor(soft, soft, wide(total), ALU.mult))
                if k == 8:
                    for n in range(12):
                        nc.vector.max(top8[:, n, :], scores_r[:, n, 0:EXPERTS])
                if k == 9:
                    for n in range(12, 16):
                        ins = nc.vector.max(top8[:, n, :], scores_r[:, n, 0:EXPERTS])
                    chain(ins)
                    chain(nc.vector.memset(top8[:, :, TOP_K:8], -1.0))
                    dve.wait_ge(r_sent, 1)
                for n in {9: range(8), 10: range(8, 16)}.get(k, ()):
                    ins = nc.vector.match_replace(marked[:, n, :], top8[:, n, :], scores_r[:, n, :], -2.0)
                if k == 10:
                    chain(ins)
                    chain(nc.vector.scalar_tensor_tensor(chosen, marked[:, :, 0:EXPERTS], -2.0, soft,
                                                         ALU.is_equal, ALU.mult))
                if k == 11:
                    chain(nc.vector.tensor_reduce(total, chosen, AX_X, ALU.add))
                    chain(nc.vector.tensor_scalar(total, total, 1e-12, None, ALU.max))
                    chain(nc.vector.reciprocal(total, total))
                    nc.vector.tensor_tensor(chosen, chosen, wide(total), ALU.mult).then_inc(weights_done, 1)

            def ffn_slot(h, r, live):
                k = 8 * h + r
                plain = isinstance(k, int) and k < PLAIN
                if live(0):
                    dve.wait_ge(silu_done, k + 1)
                    dve.wait_ge(upped, k + 1)
                    if plain:
                        if k >= 2:
                            wait_low_part(dve, k - 2)
                        nc.vector.tensor_tensor(hidden_w[:, r % 2, :], psum[:, 5, :], silu[:, r % 2, :], ALU.mult)\
                            .then_inc(hidden_w_done, 1)
                    else:
                        nc.vector.tensor_tensor(hidden[:, r % 2, :], psum[:, 5 + r % 2, :], silu[:, r % 2, :], ALU.mult)\
                            .then_inc(hidden_done, 1)
                if live(-1) and not by_pool(k - 1):
                    dve.wait_ge(hidden_hi_done, k)
                    nc.vector.tensor_tensor(hidden_lo[:, (r - 1) % 2, :], hidden_w[:, (r - 1) % 2, :],
                                            hidden_hi[:, (r - 1) % 2, :].bitcast(F32), ALU.subtract)\
                        .then_inc(hidden_lo_done, 1)
                if live(0) and not plain:
                    if r % 4 == 0:
                        dve.wait_ge(wide_in[r // 4], 16 * h - 16)
                    dve.wait_ge(hidden_done, k + 1 - PLAIN)
                    wait_low_part(dve, k - 2)
                    nc.vector.tensor_tensor(hidden_w[:, r % 2, :], weights_wide[r // 4][:, r % 4, :], hidden[:, r % 2, :], ALU.mult)\
                        .then_inc(hidden_w_done, 1)
                if plain:
                    if k == 1:
                        low_part(1, 3)
                    router(k)

            run_slots(dve, ffn_slot, ITEMS, 0, 1, peeled=3)

            def last_scale(b):
                dve.wait_ge(std_done, 2 * BATCH + b + 1)
                nc.vector.reciprocal(std[:, tiles_of(b), :], std[:, tiles_of(b), :]).then_inc(rstd_done, 1)
                dve.wait_ge(rstd_done, 2 * BATCH + b + 1)
                nc.vector.scalar_tensor_tensor(mean_var[:, tiles_of(b), 0:1], mean_var[:, tiles_of(b), 0:1], -1.0,
                                               std[:, tiles_of(b), :], ALU.mult, ALU.mult).then_inc(shift_done, 1)

            for b in range(BATCH):
                add_back(b)
                norm_stats(2, b)
                if b > 0:
                    last_scale(b - 1)
            norm_apply(2, BATCH - 1, last_normed)

        @block.gpsimd
        def _(pool):
            nc.gpsimd.memset(ident[:], 0.0).then_inc(ident_step, 1)
            pool.wait_ge(ident_step, 1)
            nc.gpsimd.affine_select(out=ident[:], in_=ident[:], compare_op=ALU.not_equal, fill=1.0, base=0,
                                    pattern=[[-1, P]], channel_multiplier=1).then_inc(ident_step, 1)
            nc.gpsimd.memset(scores_r[:, :, EXPERTS:SENT], -1.0).then_inc(r_sent, 1)
            nc.gpsimd.memset(ones_c[:], 1.0).then_inc(ones_set, 1)
            pool.wait_ge(ones_set, 1)

            def split(hi, lo, raw, step, base):
                one = ones_c[:, 0:1]
                if len(raw.shape) == 3:
                    one = one.rearrange("p (a b) -> p a b", a=1)
                nc.gpsimd.tensor_tensor(hi, raw, one.broadcast_to(list(raw.shape)), ALU.mult).then_inc(step, 1)
                pool.wait_ge(step, base + 1)
                return nc.gpsimd.tensor_tensor(lo, raw, hi.bitcast(F32), ALU.subtract)

            def stage_qk(m, n):
                pool.wait_ge(wqk_in, 16 * n + 16)
                positive(pool, (q_projected, k_projected)[m], 4 * n)
                split(wqk_hi[:, m, :], wqk_lo[:, m, :], wqk_raw[:, m, :], wq_step, 2 * n + m)\
                    .then_inc(wq_staged[m], 1)

            def stage_v(g):
                pool.wait_ge(wv_in, 16 * g + 16)
                positive(pool, v_projected[1], 4 * g)
                split(wv_hi[:], wv_lo[:], wv_raw[:], wv_step, g).then_inc(wv_staged, 1)

            stage_qk(0, 0)
            stage_qk(1, 0)
            stage_v(0)
            pool.wait_ge(rope_in, 16)

            def slot(h, r, live):
                t = 16 * h + r
                if isinstance(t, int) and t == -5:
                    pool.wait_ge(late_consts_in, LATE_CONSTS)
                    pool.wait_ge(normed, BATCH)
                    nc.gpsimd.tensor_tensor(x_tok[:], x_tok[:], bout_row[:].rearrange("p (a d) -> p a d", a=1)
                                            .broadcast_to([P, BATCH * TILES, D]), ALU.add).then_inc(resid_done, 1)
                if r % 8 == 2 and live(6):
                    stage_qk(0, 2 * h + (r // 8 + 1))
                    stage_qk(1, 2 * h + (r // 8 + 1))
                if r % 2 == 0 and live(4) and not (isinstance(t, int) and t < -2):
                    w, buf = 8 * h + (r + 4) // 2, (r + 4) // 2 % 2
                    before = 4 * h + (r + 4) // 4
                    if isinstance(t, int) and t == -2:
                        pool.wait_ge(rotated[1], 1)
                    if isinstance(t, int) and t == 0:
                        pool.wait_ge(rotated[0], 2)
                    if not (isinstance(t, int) and t < 0):
                        rotate(pool, 0, w, buf, before)
                    rotate(pool, 1, w, buf, before)
                if r == 7 and live(9):
                    stage_v(h + 1)
            run_slots(pool, slot, HEAD_SLOTS, 5, 4, body=16)

            def stage_block(h, par):
                e = 2 * h + par
                if isinstance(h, int) and h == 0:
                    pool.wait_ge(late_consts_in, LATE_CONSTS)
                else:
                    pool.wait_ge(ffn_in[par], 16 * h)
                positive(pool, downed, 4 * e - 4)
                split(ffn_hi[:, par, :, :], ffn_lo[:, par, :, :], ffn_raw[:, par, :, :], ffn_step, e)\
                    .then_inc(ffn_staged, 1)

            stage_block(0, 0)
            stage_block(0, 1)

            def ffn_slot(h, r, live):
                par = r // 4
                k = 8 * h + r
                if live(-1) and by_pool(k - 1):
                    pool.wait_ge(hidden_hi_done, k)
                    nc.gpsimd.tensor_tensor(hidden_lo[:, (r - 1) % 2, :], hidden_w[:, (r - 1) % 2, :],
                                            hidden_hi[:, (r - 1) % 2, :].bitcast(F32), ALU.subtract)\
                        .then_inc(plain_lo_done, 1)
                if r % 4 == 0 and live(4) and (not isinstance(h, int) or h > 0 or par == 1):
                    if par == 0:
                        stage_block(h, 1)
                    else:
                        stage_block(h + 1, 0)

            run_slots(pool, ffn_slot, ITEMS, 0, 0, peeled=3)


def rope_tables():
    inv_freq = (np.float32(1.0) / np.float32(10000.0) ** (np.arange(0, HEAD_DIM, 2, dtype=np.float32) / np.float32(HEAD_DIM)))
    ang = np.arange(SEQ, dtype=np.float32)[None, :] * inv_freq.astype(np.float32)[:, None]
    cos, sin = np.cos(ang), np.sin(ang)
    cos = np.concatenate([cos] * 4, 0)
    sin = np.concatenate([-sin, sin] * 2, 0)
    k = np.stack([cos, sin], 1)
    return np.ascontiguousarray(np.stack([k * np.float32(HEAD_DIM ** -0.5), k], 1).astype(np.float32))


def kernel(**inputs):
    import numpy as _np
    import concourse.bacc as _bacc
    from concourse import mybir as _mybir
    from concourse.bass_utils import run_bass_kernel_spmd as _run

    a = {k: _np.asarray(v) for k, v in inputs.items()}
    wqkv = a["L0_attn_w_qkv"].reshape(D, 3, PAIRS, P)
    wqk = wqkv[:, 0:2].transpose(0, 2, 1, 3)
    wv = wqkv[:, 2].reshape(D, GROUPS, 2 * P)
    wo = a["L0_attn_w_out"].reshape(PAIRS, 2, HEAD_DIM, D).transpose(2, 0, 1, 3)
    wo = _np.concatenate([wo, wo], 0)
    gate = _np.concatenate([a["L0_ffn_sgate_w"].reshape(SHARED, HIDDEN, D), a["L0_ffn_gate_w"]], 0).transpose(2, 0, 1)
    up = _np.concatenate([a["L0_ffn_sup_w"].reshape(SHARED, HIDDEN, D), a["L0_ffn_up_w"]], 0).transpose(2, 0, 1)
    down = _np.concatenate([a["L0_ffn_sdown_w"].reshape(D, SHARED, HIDDEN).transpose(2, 1, 0),
                            a["L0_ffn_down_w"].transpose(2, 0, 1)], 1)
    ffn = _np.stack([gate, up, down], 2)
    arrays = {
        "x": a["L0_attn_x"],
        "gamma": a["L0_attn_ln_gamma"].reshape(D, 1),
        "beta": a["L0_attn_ln_beta"].reshape(D, 1),
        "wqk": wqk,
        "wv": wv,
        "wout": wo,
        "bout": _np.broadcast_to(a["L0_attn_b_out"], (P, D)),
        "rope": rope_tables(),
        "router_w": a["L0_ffn_router_w"].T,
        "router_b": _np.broadcast_to(a["L0_ffn_router_bias"], (P, EXPERTS)),
        "ffn_w": ffn,
    }
    arrays = {f"in_{k}": _np.ascontiguousarray(v) for k, v in arrays.items()}
    nc = _bacc.Bacc("TRN2", target_bir_lowering=False, num_devices=1)
    args = [nc.dram_tensor(k, v.shape, _mybir.dt.from_np(v.dtype), kind="ExternalInput").ap()
            for k, v in arrays.items()]
    out = nc.dram_tensor("out_0", (BATCH, SEQ, D), _mybir.dt.float32, kind="ExternalOutput").ap()
    weight_store = nc.dram_tensor("weight_store", (EXPERTS, BATCH * SEQ), _mybir.dt.float32, kind="Internal").ap()
    layer_program(nc, *args, weight_store, out)
    r = _run(nc, [arrays], core_ids=[0])
    return r.results[0]["out_0"]
```
